# Optimizing a Trainium2 kernel written in Bass

```python
import numpy as np
import jax
import jax.numpy as jnp

def _softmax(x, axis=-1):
    return jax.nn.softmax(x, axis=axis)

def _gelu(x):
    return jax.nn.gelu(x, approximate=True)

def _silu(x):
    return jax.nn.silu(x)

def _sigmoid(x):
    return jax.nn.sigmoid(x)

def _layernorm(x, axis=-1, eps=1e-05):
    m = jnp.mean(x, axis=axis, keepdims=True)
    v = jnp.var(x, axis=axis, keepdims=True)
    return (x - m) / jnp.sqrt(v + eps)

def _scatter_add(tgt, idx, src, axis=0):
    return tgt.at[idx].add(src)

def _segment_sum(src, seg, n):
    return jax.ops.segment_sum(src, seg, n)
kernel_name = 'mk_sandwich_d1_jaxref_r8_258cbe'

def setup_inputs(seed: int=0):
    np.random.seed(seed)
    _w = jnp.asarray

    def _L0_attn_setup():
        import jax, jax.numpy as jnp
        import numpy as np
        EMBED_DIM = 256
        NUM_HEADS = 16
        HEAD_DIM = EMBED_DIM // NUM_HEADS
        BASE = 10000.0

        def rotate_half(x):
            half = x.shape[-1] // 2
            x1, x2 = (x[..., :half], x[..., half:])
            return jnp.concatenate([-x2, x1], axis=-1)

        def apply_rope(x, base=BASE):
            S, Dh = (x.shape[-2], x.shape[-1])
            inv_freq = 1.0 / base ** (jnp.arange(0, Dh, 2, dtype=jnp.float32) / Dh)
            t = jnp.arange(S, dtype=jnp.float32)
            freqs = jnp.einsum('i,j->ij', t, inv_freq)
            emb = jnp.concatenate([freqs, freqs], axis=-1)
            return x * jnp.cos(emb) + rotate_half(x) * jnp.sin(emb)
        key = jax.random.key(seed)
        ks = jax.random.split(key, 9)
        B, S, D = (2, 256, EMBED_DIM)
        xavier = lambda k, shape: jax.random.uniform(k, shape, jnp.float32, -1.0, 1.0) * float(np.sqrt(6.0 / (shape[0] + shape[1])))
        return {'x': jax.random.normal(ks[0], (B, S, D), jnp.float32), 'q_w': xavier(ks[1], (D, D)), 'k_w': xavier(ks[2], (D, D)), 'v_w': xavier(ks[3], (D, D)), 'q_b': jnp.zeros((D,), jnp.float32), 'k_b': jnp.zeros((D,), jnp.float32), 'v_b': jnp.zeros((D,), jnp.float32), 'out_w': xavier(ks[4], (D, D)), 'out_b': jnp.zeros((D,), jnp.float32)}
    _L0_attn_in = _L0_attn_setup()

    def _L0_ffn_setup():
        import jax, jax.numpy as jnp
        import numpy as np
        B_, S, D = (2, 256, 256)
        F_ = 1024
        R = 16
        H = 16
        HD = D // H
        MOD_SCALE = 0.1
        EPS = 1e-06

        def _rmsnorm(x, w):
            v = jnp.mean(x * x, axis=-1, keepdims=True)
            return x * jax.lax.rsqrt(v + EPS) * w

        def _attention(x, Wq, Wk, Wv, Wo):
            b, s, d = x.shape
            q = (x @ Wq.T).reshape(b, s, H, HD)
            k = (x @ Wk.T).reshape(b, s, H, HD)
            v = (x @ Wv.T).reshape(b, s, H, HD)
            scores = jnp.einsum('bqhd,bkhd->bhqk', q, k) / np.sqrt(HD).astype(np.float32)
            causal = jnp.tril(jnp.ones((s, s), bool))
            scores = jnp.where(causal, scores, jnp.finfo(scores.dtype).min)
            probs = jax.nn.softmax(scores, axis=-1)
            out = jnp.einsum('bhqk,bkhd->bqhd', probs, v).reshape(b, s, d)
            return out @ Wo.T
        key = jax.random.key(seed)
        ks = jax.random.split(key, 12)
        sd = 0.02
        return {'hidden_states': jax.random.normal(ks[0], (B_, S, D), jnp.float32), 'ln1_w': jnp.ones((D,), jnp.float32), 'ln2_w': jnp.ones((D,), jnp.float32), 'Wq': jax.random.normal(ks[1], (D, D), jnp.float32) * sd, 'Wk': jax.random.normal(ks[2], (D, D), jnp.float32) * sd, 'Wv': jax.random.normal(ks[3], (D, D), jnp.float32) * sd, 'Wo': jax.random.normal(ks[4], (D, D), jnp.float32) * sd, 'A': jax.random.normal(ks[5], (D, R), jnp.float32) * (0.01 / np.sqrt(D)), 'B': jax.random.normal(ks[6], (R, F_), jnp.float32) * (0.01 / np.sqrt(R)), 'W_in_base': jax.random.normal(ks[7], (F_, D), jnp.float32) * sd, 'W_up_base': jax.random.normal(ks[8], (F_, D), jnp.float32) * sd, 'W_down': jax.random.normal(ks[9], (D, F_), jnp.float32) * sd}
    _L0_ffn_in = _L0_ffn_setup()
    _d = {'L0_attn_x': _L0_attn_in['x'], 'L0_attn_q_w': _L0_attn_in['q_w'], 'L0_attn_k_w': _L0_attn_in['k_w'], 'L0_attn_v_w': _L0_attn_in['v_w'], 'L0_attn_q_b': _L0_attn_in['q_b'], 'L0_attn_k_b': _L0_attn_in['k_b'], 'L0_attn_v_b': _L0_attn_in['v_b'], 'L0_attn_out_w': _L0_attn_in['out_w'], 'L0_attn_out_b': _L0_attn_in['out_b'], 'L0_ffn_ln1_w': _L0_ffn_in['ln1_w'], 'L0_ffn_ln2_w': _L0_ffn_in['ln2_w'], 'L0_ffn_Wq': _L0_ffn_in['Wq'], 'L0_ffn_Wk': _L0_ffn_in['Wk'], 'L0_ffn_Wv': _L0_ffn_in['Wv'], 'L0_ffn_Wo': _L0_ffn_in['Wo'], 'L0_ffn_A': _L0_ffn_in['A'], 'L0_ffn_B': _L0_ffn_in['B'], 'L0_ffn_W_in_base': _L0_ffn_in['W_in_base'], 'L0_ffn_W_up_base': _L0_ffn_in['W_up_base'], 'L0_ffn_W_down': _L0_ffn_in['W_down']}
    _x0 = _d['L0_attn_x']
    _d['L0_attn_x'] = jax.random.normal(jax.random.fold_in(jax.random.key(seed), 1), (4, 1024, 256), dtype=_x0.dtype)
    del _x0
    return _d

def reference(L0_attn_x, L0_attn_q_w, L0_attn_k_w, L0_attn_v_w, L0_attn_q_b, L0_attn_k_b, L0_attn_v_b, L0_attn_out_w, L0_attn_out_b, L0_ffn_ln1_w, L0_ffn_ln2_w, L0_ffn_Wq, L0_ffn_Wk, L0_ffn_Wv, L0_ffn_Wo, L0_ffn_A, L0_ffn_B, L0_ffn_W_in_base, L0_ffn_W_up_base, L0_ffn_W_down):

    def _L0_attn_ref(x, q_w, k_w, v_w, q_b, k_b, v_b, out_w, out_b):
        import jax, jax.numpy as jnp
        import numpy as np
        EMBED_DIM = 256
        NUM_HEADS = 16
        HEAD_DIM = EMBED_DIM // NUM_HEADS
        BASE = 10000.0

        def rotate_half(x):
            half = x.shape[-1] // 2
            x1, x2 = (x[..., :half], x[..., half:])
            return jnp.concatenate([-x2, x1], axis=-1)

        def apply_rope(x, base=BASE):
            S, Dh = (x.shape[-2], x.shape[-1])
            inv_freq = 1.0 / base ** (jnp.arange(0, Dh, 2, dtype=jnp.float32) / Dh)
            t = jnp.arange(S, dtype=jnp.float32)
            freqs = jnp.einsum('i,j->ij', t, inv_freq)
            emb = jnp.concatenate([freqs, freqs], axis=-1)
            return x * jnp.cos(emb) + rotate_half(x) * jnp.sin(emb)
        B, S, D = x.shape
        H, Dh = (NUM_HEADS, HEAD_DIM)
        scaling = Dh ** (-0.5)
        q = (x @ q_w.T + q_b).reshape(B, S, H, Dh).transpose(0, 2, 1, 3)
        k = (x @ k_w.T + k_b).reshape(B, S, H, Dh).transpose(0, 2, 1, 3)
        v = (x @ v_w.T + v_b).reshape(B, S, H, Dh).transpose(0, 2, 1, 3)
        q = apply_rope(q)
        k = apply_rope(k)
        attn = jnp.einsum('bhqd,bhkd->bhqk', q, k) * scaling
        probs = jax.nn.softmax(attn, axis=-1)
        out = jnp.einsum('bhqk,bhkd->bhqd', probs, v)
        out = out.transpose(0, 2, 1, 3).reshape(B, S, D)
        return out @ out_w.T + out_b

    def _L0_ffn_ref(hidden_states, ln1_w, ln2_w, Wq, Wk, Wv, Wo, A, B, W_in_base, W_up_base, W_down):
        import jax, jax.numpy as jnp
        import numpy as np
        B_, S, D = (2, 256, 256)
        F_ = 1024
        R = 16
        H = 16
        HD = D // H
        MOD_SCALE = 0.1
        EPS = 1e-06

        def _rmsnorm(x, w):
            v = jnp.mean(x * x, axis=-1, keepdims=True)
            return x * jax.lax.rsqrt(v + EPS) * w

        def _attention(x, Wq, Wk, Wv, Wo):
            b, s, d = x.shape
            q = (x @ Wq.T).reshape(b, s, H, HD)
            k = (x @ Wk.T).reshape(b, s, H, HD)
            v = (x @ Wv.T).reshape(b, s, H, HD)
            scores = jnp.einsum('bqhd,bkhd->bhqk', q, k) / np.sqrt(HD).astype(np.float32)
            causal = jnp.tril(jnp.ones((s, s), bool))
            scores = jnp.where(causal, scores, jnp.finfo(scores.dtype).min)
            probs = jax.nn.softmax(scores, axis=-1)
            out = jnp.einsum('bhqk,bkhd->bqhd', probs, v).reshape(b, s, d)
            return out @ Wo.T
        residual = hidden_states
        x = _rmsnorm(hidden_states, ln1_w)
        attn = _attention(x, Wq, Wk, Wv, Wo)
        mod = MOD_SCALE * jnp.tanh(attn @ A)
        h = _rmsnorm(residual, ln2_w)
        gate_pre = h @ W_in_base.T + mod * (h @ A) @ B
        gate = jax.nn.silu(gate_pre)
        up = h @ W_up_base.T
        mlp_out = gate * up @ W_down.T
        return residual + mlp_out
    x = L0_attn_x
    x = x + _layernorm(_L0_attn_ref(_layernorm(x, axis=-1), L0_attn_q_w, L0_attn_k_w, L0_attn_v_w, L0_attn_q_b, L0_attn_k_b, L0_attn_v_b, L0_attn_out_w, L0_attn_out_b), axis=-1)
    x = x + _layernorm(_L0_ffn_ref(_layernorm(x, axis=-1), L0_ffn_ln1_w, L0_ffn_ln2_w, L0_ffn_Wq, L0_ffn_Wk, L0_ffn_Wv, L0_ffn_Wo, L0_ffn_A, L0_ffn_B, L0_ffn_W_in_base, L0_ffn_W_up_base, L0_ffn_W_down), axis=-1)
    return x

_drawn_inputs = setup_inputs


def setup_inputs(seed=0):
    import zlib

    import numpy as np

    out = dict(_drawn_inputs(seed))
    spreads = {'L0_attn_q_b': (0.0, 0.1),
     'L0_attn_k_b': (0.0, 0.1),
     'L0_attn_v_b': (0.0, 0.1),
     'L0_attn_out_b': (0.0, 0.1),
     'L0_ffn_ln1_w': (1.0, 0.6),
     'L0_ffn_ln2_w': (1.0, 0.6)}
    factors = {'L0_ffn_Wq': 200.0,
     'L0_ffn_Wk': 200.0,
     'L0_ffn_Wv': 196.617,
     'L0_ffn_Wo': 198.376,
     'L0_ffn_A': 200.0,
     'L0_ffn_B': 194.685,
     'L0_ffn_W_in_base': 3.56,
     'L0_ffn_W_up_base': 3.511,
     'L0_ffn_W_down': 3.533}
    for name, (base, spread) in spreads.items():
        noise = np.random.default_rng([zlib.crc32(name.encode()), seed]).standard_normal(out[name].shape)
        drawn = base * np.exp(spread * noise) if base else spread * noise
        out[name] = jnp.asarray(drawn.astype(out[name].dtype))
    for name, factor in factors.items():
        out[name] = (out[name] * factor).astype(out[name].dtype)
    return out
```

```python
from contextlib import ExitStack

import numpy as np

import concourse.bass as bass
from concourse import mybir

F32 = mybir.dt.float32
BF16 = mybir.dt.bfloat16
ALU = mybir.AluOpType
ACT = mybir.ActivationFunctionType
AX = mybir.AxisListType

P = 128
B, S, D = 4, 1024, 256
H, HD = 16, 16
F = 1024
R = 16
KC = D // P
FC = F // P
CH = 512
CT = CH // P
HALVES = S // CH
GH = 4
GROUPS = B * H // GH
GD = GH * HD
NG = H // GH
ST = S // P
VW = 32
PARTS = 3
Q_PARTS = [0, 0, 1, 1, 0, 2]
K_PARTS = [0, 1, 0, 1, 2, 0]
SROWS = HD * len(Q_PARTS)
AROWS = SROWS + 2
SETS = 3
SCALE = HD ** -0.5
AHEAD = 2
LN_EPS, RMS_EPS = 1e-5, 1e-6
MOD_SCALE = 0.1
MASKED = -1e30


class Program:

    def __init__(self, nc, ctx, a, out):
        self.nc, self.ctx, self.a, self.out = nc, ctx, a, out

    def sb(self, name, shape, dt=F32, ctx=None):
        return (ctx or self.ctx).enter_context(self.nc.sbuf_tensor(name, shape, dt))

    def ps(self, name, shape, ctx, dt=F32):
        return ctx.enter_context(self.nc.psum_tensor(name, shape, dt))

    def sem(self, name):
        return self.ctx.enter_context(self.nc.semaphore(name))


def build(nc, a, out):
    with ExitStack() as ctx:
        p = Program(nc, ctx, a, out)
        p.q_scr = [nc.dram_tensor(f"q_scr{n}", (PARTS, B * D, S), BF16, kind="Internal").ap() for n in range(2)]
        p.k_scr = [nc.dram_tensor(f"k_scr{n}", (PARTS, B * D, S), BF16, kind="Internal").ap() for n in range(2)]
        p.v_scr = [nc.dram_tensor(f"v_scr{n}", (GROUPS, S, GH * VW), F32, kind="Internal").ap() for n in range(2)]
        p.att_scr = [nc.dram_tensor(f"att_scr{n}", (GROUPS, S, GD), F32, kind="Internal").ap() for n in range(2)]
        p.u_scr = nc.dram_tensor("u_scr", (B * S, D), F32, kind="Internal").ap()
        p.zT_scr = nc.dram_tensor("zT_scr", (D, B * S), F32, kind="Internal").ap()
        p.ident = p.sb("ident", [P, P])
        p.ident_bf = p.sb("ident_bf", [P, P], BF16)
        p.causal = p.sb("causal", [P, 2, P], BF16)
        p.eps = p.sb("eps", [P, 2])
        p.x_all = p.sb("x_all", [P, B * ST, D])
        p.waits_apart = p.sem("waits_apart")
        constants(p)
        project_rope(p)
        attention(p, 0, causal=False)
        project_ffn(p)
        attention(p, 1, causal=True)
        feed_forward(p)


def constants(p):
    nc = p.nc
    zeroed, shaped = p.sem("const_zeroed"), p.sem("constants_shaped")
    with nc.Block() as block:
        @block.gpsimd
        def _(pool):
            nc.gpsimd.memset(p.ident[:], 0.0).then_inc(zeroed, 1)
            nc.gpsimd.memset(p.ident_bf[:], 0.0).then_inc(zeroed, 1)
            nc.gpsimd.memset(p.causal[:], 0.0).then_inc(zeroed, 1)
            nc.gpsimd.memset(p.eps[:, 0:1], LN_EPS).then_inc(zeroed, 1)
            nc.gpsimd.memset(p.eps[:, 1:2], RMS_EPS).then_inc(zeroed, 1)
            pool.wait_ge(zeroed, 5)
            for m in (p.ident, p.ident_bf):
                nc.gpsimd.affine_select(out=m[:], in_=m[:], compare_op=ALU.not_equal, fill=1.0, base=0,
                                        pattern=[[-1, P]], channel_multiplier=1).then_inc(shaped, 1)
            for form, step in ((0, -1), (1, 1)):
                nc.gpsimd.affine_select(out=p.causal[:, form, :], in_=p.causal[:, form, :], compare_op=ALU.is_ge, fill=MASKED, base=0,
                                        pattern=[[step, P]], channel_multiplier=-step).then_inc(shaped, 1)
            pool.wait_ge(shaped, 4)


def wait_apart(p, eng, sem, value):
    eng.wait_ge(sem, value)
    eng.sem_inc(p.waits_apart, 1)


def rows_in(w):
    return w.rearrange("(k p) n -> p k n", p=P)


def store_v(sp, scr, b, h, vout, stored):
    for hg in range(NG):
        sp.dma_start(scr[bass.ds(b * NG + hg, 1), h * CH:(h + 1) * CH, :].rearrange("o (t p) c -> p (o t) c", p=P),
                     vout[:, :, hg * GH:(hg + 1) * GH, :].rearrange("p t h c -> p t (h c)")).then_inc(stored, 16)


def project_rope(p):
    nc, a = p.nc, p.a
    with ExitStack() as ctx:
        def sb(name, shape, dt=F32):
            return p.sb("r_" + name, shape, dt, ctx)

        def sem(name):
            return p.sem("r_" + name)

        w = {n: sb(f"w_{n}", [P, KC, D]) for n in ("q", "qr", "k", "kr", "v")}
        bias = sb("bias", [P, 4, KC])
        vbias = sb("vbias", [P, D])
        cos, sin = sb("cos", [P, S]), sb("sin", [P, S])
        stats = [sb(f"stats{h}", [P, CT, 6]) for h in range(2)]
        mv = [sb(f"mv{h}", [P, CT, 2]) for h in range(2)]
        sd = [sb(f"sd{h}", [P, CT]) for h in range(2)]
        rstd = [sb(f"rstd{h}", [P, CT]) for h in range(2)]
        xn = [sb(f"xn{h}", [P, CT, D]) for h in range(2)]
        xnT = [sb(f"xnT{h}", [P, KC, CH]) for h in range(2)]
        t_cos = [sb(f"tcos{u}", [P, CH]) for u in range(2)]
        t_sin = [sb(f"tsin{u}", [P, CH]) for u in range(2)]
        t_sum = [sb(f"tsum{u}", [P, CH]) for u in range(2)]
        rest = [sb(f"rest{u}", [P, CH]) for u in range(2)]
        parts = [sb(f"parts{u}", [P, PARTS, CH], BF16) for u in range(2)]
        vout = [sb(f"v{h}", [P, CT, H, VW]) for h in range(2)]
        t_ps = p.ps("r_t_ps", [P, KC, CH], ctx)
        pair_ps = [p.ps(f"r_pair_ps{u}", [P, 2, CH], ctx) for u in range(2)]
        v_ps = p.ps("r_v_ps", [P, CT, D], ctx)

        w_in, x_in = sem("w_in"), [sem(f"x_in{b}") for b in range(B)]
        stats_done, mv_done, sd_done, rstd_done, xn_done = (sem(n) for n in ("stats_done", "mv_done", "sd_done", "rstd_done", "xn_done"))
        t_done, xnT_done, pair_done = sem("t_done"), sem("xnT_done"), sem("pair_done")
        cos_done, sin_done, sum_done, rest_done = sem("cos_done"), sem("sin_done"), sem("sum_done"), sem("rest_done")
        part_done = [sem(f"part{n}_done") for n in range(PARTS)]
        v_done, v_copied, v_ones = sem("v_done"), sem("v_copied"), sem("v_ones")
        parts_free = [sem(f"parts_free{u}") for u in range(2)]
        vout_free = [sem(f"vout_free{h}") for h in range(2)]
        UC = 2 * KC
        UB = UC * HALVES
        N_LOADS = 9

        def chunk(b, h):
            return b * HALVES + h

        def unit(b, h, u):
            return b * UB + (h * UC + u)

        with nc.Block() as block:
            @block.sync
            def _(sp):
                for b in range(B):
                    sp.dma_start(p.x_all[:, b * ST:(b + 1) * ST, :],
                                 a["x"][b * S:(b + 1) * S, :].rearrange("(t p) c -> p t c", p=P)).then_inc(x_in[b], 16)
                for u in range(2):
                    sp.sem_inc(parts_free[u], 16)
                    sp.sem_inc(vout_free[u], 16 * NG)
                with sp.Fori(0, B) as b:
                    for h in range(HALVES):
                        for u in range(UC):
                            m = u % KC
                            scr = (p.q_scr if u < KC else p.k_scr)[0]
                            wait_apart(p, sp, part_done[2], unit(b, h, u) + 1)
                            sp.dma_start(scr[:, bass.ds(b * D + m * P, P), h * CH:(h + 1) * CH].rearrange("a r t -> r a t"),
                                         parts[u % 2][:]).then_inc(parts_free[u % 2], 16)
                        wait_apart(p, sp, v_copied, CT * (chunk(b, h) + 2))
                        store_v(sp, p.v_scr[0], b, h, vout[h], vout_free[h])
                for u in range(2):
                    wait_apart(p, sp, parts_free[u], 16 * (B * UB // 2 + 1))
                    wait_apart(p, sp, vout_free[u], 16 * NG * (B + 1))

            @block.gpsimd
            def _(pool):
                for h in range(2):
                    nc.gpsimd.memset(vout[h][:], 1.0).then_inc(v_ones, 1)
                pool.sem_inc(sum_done, AHEAD)
                with pool.Fori(0, B) as b:
                    for h in range(HALVES):
                        for u in range(UC):
                            k, n = u % 2, unit(b, h, u)
                            pool.wait_ge(cos_done, n + 1)
                            pool.wait_ge(sin_done, n + 1 + AHEAD)
                            nc.gpsimd.tensor_tensor(t_sum[k][:], t_cos[k][:], t_sin[k][:], ALU.add).then_inc(sum_done, 1)
                            pool.wait_ge(part_done[0], n + 1)
                            nc.gpsimd.tensor_tensor(rest[k][:], t_sum[k][:], parts[k][:, 0, :], ALU.subtract).then_inc(rest_done, 1)
                            pool.wait_ge(part_done[1], n + 1)
                            nc.gpsimd.tensor_tensor(parts[k][:, 2, :], rest[k][:], parts[k][:, 1, :], ALU.subtract).then_inc(part_done[2], 1)

            @block.scalar
            def _(act):
                for n in ("q", "qr", "k", "kr", "v"):
                    act.dma_start(w[n][:], rows_in(a["w_" + n])).then_inc(w_in, 16)
                for t, n in ((bias, "qk_bias"), (cos, "cos"), (sin, "sin"), (vbias, "v_bias")):
                    act.dma_start(t[:], a[n]).then_inc(w_in, 16)

                def roots(b):
                    for h in range(HALVES):
                        act.wait_ge(mv_done, CT * (chunk(b, h) + 1))
                        nc.scalar.activation(sd[h][:], mv[h][:, :, 1], ACT.Sqrt, bias=p.eps[:, 0:1]).then_inc(sd_done, 1)

                def split(b, h):
                    act.wait_ge(t_done, chunk(b, h) + 1 + AHEAD)
                    nc.scalar.copy(xnT[h][:], t_ps[:]).then_inc(xnT_done, 1)
                    for u in range(UC):
                        k, n = u % 2, unit(b, h, u)
                        act.wait_ge(parts_free[k], 16 * (b * (UB // 2) + h * (UC // 2) + u // 2 + 1))
                        act.wait_ge(sum_done, n + 1 + AHEAD)
                        nc.scalar.copy(parts[k][:, 0, :], t_sum[k][:]).then_inc(part_done[0], 1)
                        act.wait_ge(rest_done, n + 1)
                        nc.scalar.copy(parts[k][:, 1, :], rest[k][:]).then_inc(part_done[1], 1)

                act.sem_inc(xnT_done, 1)
                roots(0)
                with act.Fori(0, B - 1) as b:
                    split(b, 0)
                    roots(b + 1)
                    split(b, 1)
                split(B - 1, 0)
                split(B - 1, 1)

            @block.vector
            def _(dve):
                def norm(b, h):
                    n = chunk(b, h)
                    for t in range(CT):
                        nc.vector.bn_stats(stats[h][:, t, :], p.x_all[:, bass.ds(n * CT + t, 1), :].rearrange("p o c -> p (o c)")).then_inc(stats_done, 1)
                    wait_apart(p, dve, stats_done, CT * (n + 1))
                    for t in range(CT):
                        nc.vector.bn_aggr(mv[h][:, t, :], stats[h][:, t, :]).then_inc(mv_done, 1)

                def normed(b, h):
                    n = chunk(b, h)
                    dve.wait_ge(sd_done, n + 1)
                    nc.vector.reciprocal(rstd[h][:], sd[h][:]).then_inc(rstd_done, 1)
                    dve.wait_ge(rstd_done, n + 1)
                    dve.wait_ge(t_done, n + 1)
                    for t in range(CT):
                        nc.vector.tensor_scalar(xn[h][:, t, :], p.x_all[:, bass.ds(n * CT + t, 1), :].rearrange("p o c -> p (o c)"),
                                                mv[h][:, t, 0:1], rstd[h][:, t:t + 1], ALU.subtract, ALU.mult).then_inc(xn_done, 1)

                def rope(b, h):
                    cols = slice(h * CH, (h + 1) * CH)
                    for u in range(UC):
                        k, n, m, j = u % 2, unit(b, h, u), u % KC, 2 * (u // KC)
                        dve.wait_ge(pair_done, n + 1)
                        dve.wait_ge(sum_done, n + 1)
                        nc.vector.scalar_tensor_tensor(t_cos[k][:], pair_ps[k][:, 0, :], bias[:, j, m:m + 1], cos[:, cols],
                                                       ALU.add, ALU.mult).then_inc(cos_done, 1)
                        nc.vector.scalar_tensor_tensor(t_sin[k][:], pair_ps[k][:, 1, :], bias[:, j + 1, m:m + 1], sin[:, cols],
                                                       ALU.add, ALU.mult).then_inc(sin_done, 1)
                    dve.wait_ge(v_done, chunk(b, h) + 1)
                    dve.wait_ge(vout_free[h], 16 * NG * (b + 1))
                    for t in range(CT):
                        nc.vector.tensor_tensor(vout[h][:, t, :, 0:HD], v_ps[:, t, :].rearrange("p (h c) -> p h c", c=HD),
                                                vbias[:].rearrange("p (h c) -> p h c", c=HD), ALU.add).then_inc(v_copied, 1)

                dve.sem_inc(sin_done, AHEAD)
                dve.sem_inc(v_copied, CT)
                dve.wait_ge(v_ones, 2)
                for b in range(B):
                    dve.wait_ge(x_in[b], 16)
                for h in range(HALVES):
                    norm(0, h)
                for h in range(HALVES):
                    normed(0, h)
                dve.wait_ge(w_in, 16 * N_LOADS)
                with dve.Fori(0, B - 1) as b:
                    rope(b, 0)
                    for h in range(HALVES):
                        norm(b + 1, h)
                    normed(b + 1, 0)
                    rope(b, 1)
                    normed(b + 1, 1)
                rope(B - 1, 0)
                rope(B - 1, 1)

            @block.tensor
            def _(pe):
                pe.sem_inc(t_done, AHEAD)
                pe.wait_ge(w_in, 16 * N_LOADS)

                def project(b, h):
                    n = chunk(b, h)
                    pe.wait_ge(xn_done, CT * (n + 1))
                    pe.wait_ge(xnT_done, n + 1)
                    for kc in range(KC):
                        for t in range(CT):
                            last = nc.tensor.transpose(t_ps[:, kc, t * P:(t + 1) * P], xn[h][:, t, kc * P:(kc + 1) * P], p.ident[:])
                    last.then_inc(t_done, 1)
                    pe.wait_ge(xnT_done, n + 2)
                    pe.wait_ge(v_copied, CT * (n + 1))
                    for t in range(CT):
                        for kc in range(KC):
                            last = nc.tensor.matmul(v_ps[:, t, :], xnT[h][:, kc, t * P:(t + 1) * P], w["v"][:, kc, :],
                                                    start=kc == 0, stop=kc == KC - 1)
                    last.then_inc(v_done, 1)
                    for u in range(UC):
                        m, names = u % KC, (("q", "qr") if u < KC else ("k", "kr"))
                        pe.wait_ge(sin_done, unit(b, h, u) + 1)
                        for j, name in enumerate(names):
                            for kc in range(KC):
                                last = nc.tensor.matmul(pair_ps[u % 2][:, j, :], w[name][:, kc, m * P:(m + 1) * P], xnT[h][:, kc, :],
                                                        start=kc == 0, stop=kc == KC - 1)
                        last.then_inc(pair_done, 1)

                with pe.Fori(0, B) as b:
                    project(b, 0)
                    project(b, 1)


def attention(p, layer, causal):
    nc = p.nc
    q_scr, k_scr, v_scr, att_scr = p.q_scr[layer], p.k_scr[layer], p.v_scr[layer], p.att_scr[layer]
    with ExitStack() as ctx:
        def sb(name, shape, dt=F32):
            return p.sb(f"a{layer}_" + name, shape, dt, ctx)

        def sem(name):
            return p.sem(f"a{layer}_" + name)

        qa = [sb(f"q{s}", [AROWS, GH, S], BF16) for s in range(SETS)]
        ka = [sb(f"k{s}", [AROWS, GH, S], BF16) for s in range(SETS)]
        va = [sb(f"v{s}", [P, ST, GH, VW]) for s in range(SETS)]
        probs = [sb(f"p{j}", [P, GH, S]) for j in range(2)]
        row_max = [sb(f"rmax{s}", [P, GH, ST]) for s in range(SETS)]
        neg_max = sb("negmax", [GH * ST, 2, P], BF16)
        o_sb = sb("o", [P, S])
        rden = sb("rden", [P, ST * GH])
        o_out = sb("oout", [P, ST * GH, HD])
        ring = [p.ps(f"a{layer}_ring{j}", [P, S], ctx) for j in range(2)]
        s_ps = [p.ps(f"a{layer}_s{j}", [P, CH], ctx) for j in range(2)]
        o_ps = p.ps(f"a{layer}_o_ps", [P, S], ctx)

        loaded, ones_set = [sem(f"loaded{s}") for s in range(SETS)], sem("ones_set")
        ring_full, ring_free = sem("ring_full"), sem("ring_free")
        neg_hi_done, neg_in = sem("neg_hi_done"), sem("neg_in")
        s_full, exp_done, pv_done = sem("s_full"), sem("exp_done"), sem("pv_done")
        o_copied, rden_done, stored = sem("o_copied"), sem("rden_done"), sem("stored")

        LOADS = 2 * len(Q_PARTS) + 1
        STEPS = ST * GH
        TURN = 2 * GH
        SCORES = GH * ST
        LEAD = 12 if causal else 6
        MAX_AT = STEPS - LEAD
        OUT_AT = GH + 2
        RG = SCORES + 2
        assert RG % 2 == 0

        def first_q(kt):
            return kt * P if causal else 0

        def banks_of(kt):
            return [(c, max(first_q(kt), c * CH), (c + 1) * CH) for c in range(HALVES) if first_q(kt) < (c + 1) * CH]

        exp_no, add_no = {}, {}
        for kt in range(ST):
            for c, _, _ in banks_of(kt):
                add_no[kt, c] = len(add_no)
            for h in range(GH):
                for c, _, _ in banks_of(kt):
                    exp_no[kt, h, c] = len(exp_no)
        EXPS, ADDS = len(exp_no), len(add_no)
        EXPS_UNTIL = [1 + max(n for (kt, _, _), n in exp_no.items() if kt <= last) for last in range(ST)]
        assert EXPS % 2 == 0

        EARLY = LEAD + TURN
        START = SCORES + 1 + EARLY
        body_steps = list(range(TURN, STEPS)) + list(range(TURN))

        def units_of(n, inner):
            units = [("score", n + LEAD) if n < MAX_AT and inner else ("next", n - MAX_AT if inner else n + LEAD)]
            if n % 2 and n - 1 == MAX_AT:
                units.append(("max", 0))
            if n % 2 and n - 1 == OUT_AT:
                units.append(("out", 0))
            return units

        in_body = [unit for j, n in enumerate(body_steps) for unit in units_of(n, j < STEPS - TURN)]
        place = {unit: n for n, unit in enumerate(in_body)}
        in_last = [unit for unit in in_body if unit[0] != "next"]
        last_place = {unit: n for n, unit in enumerate(in_last)}
        assert len(in_body) == RG and LEAD % 2 == 0 and TURN % 2 == 0

        END = START + (GROUPS - 2) * RG + len(in_last)

        def slot(number):
            return ring[number % 2]

        with nc.Block() as block:
            @block.sync
            def _(sp):
                def load(g, s):
                    rows = bass.ds(g * GD, GD)
                    for j in range(len(Q_PARTS)):
                        for t, scr, part in ((qa[s], q_scr, Q_PARTS[j]), (ka[s], k_scr, K_PARTS[j])):
                            sp.dma_start(t[j * HD:(j + 1) * HD, :, :],
                                         scr[part, rows, :].rearrange("(h d) t -> d h t", d=HD)).then_inc(loaded[s], 16)
                    sp.dma_start(va[s][:].rearrange("p t h c -> p t (h c)"),
                                 v_scr[bass.ds(g, 1), :, :].rearrange("o (t p) c -> p (o t) c", p=P)).then_inc(loaded[s], 16)

                def place_max(units_before, s):
                    wait_apart(p, sp, ring_free, units_before + 1 + AHEAD)
                    for j in range(2):
                        sp.dma_start(qa[s][SROWS + j:SROWS + j + 1, :, :].rearrange("o h (t q) -> o (h t) q", q=P),
                                     neg_max[:, j, :]).then_inc(neg_in, 16)

                def store(g, units_before):
                    wait_apart(p, sp, ring_free, units_before + 1 + AHEAD)
                    sp.dma_start(att_scr[bass.ds(g, 1), :, :].rearrange("o (t p) c -> p (o t) c", p=P),
                                 o_out[:].rearrange("p (t h) c -> p t (h c)", h=GH)).then_inc(stored, 16)

                def body(g, k, more, where):
                    place_max(START + g * RG + where["max", 0], (k + 1) % SETS)
                    if more:
                        wait_apart(p, sp, pv_done, ADDS * (g + 1))
                        load(g + SETS, k)
                    store(g, START + g * RG + where["out", 0])

                sp.sem_inc(stored, 16)
                sp.sem_inc(neg_in, 32)
                for g in range(SETS):
                    load(g, g)
                place_max(SCORES, 0)
                with sp.Fori(0, (GROUPS - SETS) // SETS) as i:
                    for k in range(SETS):
                        body(i * SETS + k, k, True, place)
                for g in range((GROUPS - SETS) // SETS * SETS, GROUPS - 1):
                    body(g, g % SETS, g + SETS < GROUPS, last_place if g == GROUPS - 2 else place)
                store(GROUPS - 1, END)
                sp.wait_ge(stored, 16 * (GROUPS + 1))

            @block.gpsimd
            def _(pool):
                for s in range(SETS):
                    nc.gpsimd.memset(ka[s][SROWS:AROWS, :, :], 1.0).then_inc(ones_set, 1)

            @block.scalar
            def _(act):
                def exps(g, kt, before=None, heads=range(GH)):
                    if heads[0] == 0 and kt >= 2:
                        act.wait_ge(pv_done, ADDS * g + add_no[kt - 2, HALVES - 1] + 1)
                    elif heads[0] == 0 and before is not None:
                        act.wait_ge(pv_done, ADDS * before + add_no[ST - 2 + kt, HALVES - 1] + 1)
                    for h in heads:
                        for c, lo, hi in banks_of(kt):
                            n = exp_no[kt, h, c]
                            act.wait_ge(s_full, EXPS * g + n + 1)
                            nc.scalar.activation(probs[kt % 2][:, h, lo:hi], s_ps[n % 2][:, lo - c * CH:hi - c * CH], ACT.Exp,
                                                 scale=SCALE).then_inc(exp_done, 1)

                def copy_o(g, c):
                    kt = max(kt for kt, bank in add_no if bank == c)
                    act.wait_ge(pv_done, ADDS * g + add_no[kt, c] + 1)
                    nc.scalar.copy(o_sb[:, c * CH:(c + 1) * CH], o_ps[:, c * CH:(c + 1) * CH]).then_inc(o_copied, 1)

                act.sem_inc(exp_done, AHEAD)
                act.sem_inc(o_copied, HALVES)
                exps(0, 0)
                exps(0, 1)
                with act.Fori(0, GROUPS - 1) as g:
                    for kt in range(2, ST):
                        exps(g, kt)
                    exps(g + 1, 0, g)
                    copy_o(g, 0)
                    exps(g + 1, 1, g, range(2))
                    copy_o(g, 1)
                    exps(g + 1, 1, g, range(2, GH))
                for kt in range(2, ST):
                    exps(GROUPS - 1, kt)
                for c in range(HALVES):
                    copy_o(GROUPS - 1, c)

            @block.vector
            def _(dve):
                def maximum(s, u, number, ps):
                    qt, h = divmod(u, GH)
                    dve.wait_ge(ring_full, number + 1)
                    width = (qt + 1) * P if causal else S
                    nc.vector.tensor_reduce(row_max[s][:, h, qt:qt + 1], ps[:, 0:width], AX.X, ALU.max).then_inc(ring_free, 1)

                def negate(g_of, number, ps):
                    dve.wait_ge(ring_full, number + 1)
                    dve.wait_ge(neg_in, 32 * (g_of + 1))
                    nc.vector.tensor_scalar(neg_max[:, 0, :], ps[0:GH * ST, 0:P], -1.0, None, ALU.mult).then_inc(neg_hi_done, 1)
                    dve.wait_ge(neg_hi_done, g_of + 1)
                    nc.vector.scalar_tensor_tensor(neg_max[:, 1, :], ps[0:GH * ST, 0:P], -1.0, neg_max[:, 0, :],
                                                   ALU.mult, ALU.subtract).then_inc(ring_free, 1)

                def divide(g, number, ps):
                    o_t = ps[:].rearrange("p (n c) -> p n c", c=VW)
                    dve.wait_ge(ring_full, number + 1)
                    dve.wait_ge(stored, 16 * (g + 1))
                    nc.vector.reciprocal(rden[:], o_t[:, :, HD]).then_inc(rden_done, 1)
                    dve.wait_ge(rden_done, g + 1)
                    nc.vector.tensor_tensor(o_out[:], o_t[:, :, 0:HD], rden[:].unsqueeze(2).to_broadcast([P, ST * GH, HD]),
                                            ALU.mult).then_inc(ring_free, 1)

                def body(g, k, units):
                    sets = {"score": (k + 1) % SETS, "next": (k + 2) % SETS}
                    for n, (kind, u) in enumerate(units):
                        number, ps = START + g * RG + n, slot(START + n)
                        if kind == "max":
                            negate(g + 1, number, ps)
                        elif kind == "out":
                            divide(g, number, ps)
                        else:
                            maximum(sets[kind], u, number, ps)

                dve.sem_inc(ring_free, AHEAD)
                for u in range(SCORES):
                    maximum(0, u, u, slot(u))
                negate(0, SCORES, slot(SCORES))
                for u in range(EARLY):
                    maximum(1, u, SCORES + 1 + u, slot(SCORES + 1 + u))
                with dve.Fori(0, (GROUPS - SETS) // SETS) as i:
                    for k in range(SETS):
                        body(i * SETS + k, k, in_body)
                for g in range((GROUPS - SETS) // SETS * SETS, GROUPS - 1):
                    body(g, g % SETS, in_last if g == GROUPS - 2 else in_body)
                divide(GROUPS - 1, END, slot(END))

            @block.tensor
            def _(pe):
                def score(s, u, number, ps):
                    qt, h = divmod(u, GH)
                    width = (qt + 1) * P if causal else S
                    pe.wait_ge(ring_free, number + 1)
                    for lo in range(0, width, CH):
                        hi = min(width, lo + CH)
                        diagonal = causal and hi == width
                        last = nc.tensor.matmul(ps[:, lo:hi], qa[s][0:SROWS, h, qt * P:(qt + 1) * P], ka[s][0:SROWS, h, lo:hi],
                                                start=True, stop=not diagonal)
                    if causal:
                        last = nc.tensor.matmul(ps[:, width - P:width], p.ident_bf[:], p.causal[:, 0, :], start=False, stop=True)
                    last.then_inc(ring_full, 1)

                def turn_max(s, number, ps, read):
                    pe.wait_ge(ring_free, read + AHEAD)
                    pe.wait_ge(ring_free, number + 1)
                    nc.tensor.transpose(ps[0:GH * ST, 0:P], row_max[s][:].rearrange("p h t -> p (h t)"), p.ident[:]).then_inc(ring_full, 1)

                def turn_out(g, number, ps):
                    pe.wait_ge(o_copied, HALVES * (g + 2))
                    pe.wait_ge(ring_free, number + 1)
                    for t in range(ST):
                        last = nc.tensor.transpose(ps[:, t * P:(t + 1) * P], o_sb[:, t * P:(t + 1) * P], p.ident[:])
                    last.then_inc(ring_full, 1)

                def weigh(g, s, kt, c):
                    for bank, lo, hi in banks_of(kt):
                        if bank != c:
                            continue
                        pe.wait_ge(exp_done, EXPS * g + EXPS_UNTIL[kt] + AHEAD)
                        if kt == 0:
                            pe.wait_ge(o_copied, HALVES * g + c + 1)
                        for h in range(GH):
                            last = nc.tensor.matmul(o_ps[h * VW:(h + 1) * VW, lo:hi], va[s][:, kt, h, :], probs[kt % 2][:, h, lo:hi],
                                                    start=kt == 0, stop=kt == (hi // P - 1 if causal else ST - 1))
                        last.then_inc(pv_done, 1)

                def keys_by_queries(g, s, n):
                    kt, h = divmod(n, GH)
                    if n == 0:
                        pe.wait_ge(neg_in, 32 * (g + 2))
                    for c, lo, hi in banks_of(kt):
                        m = exp_no[kt, h, c]
                        pe.wait_ge(exp_done, EXPS * g + m + 1)
                        diagonal = causal and lo == kt * P
                        last = nc.tensor.matmul(s_ps[m % 2][:, lo - c * CH:hi - c * CH], ka[s][:, h, kt * P:(kt + 1) * P],
                                                qa[s][:, h, lo:hi], start=True, stop=not diagonal)
                        if diagonal:
                            last = nc.tensor.matmul(s_ps[m % 2][:, lo - c * CH:lo - c * CH + P], p.ident_bf[:], p.causal[:, 1, :],
                                                    start=False, stop=True)
                        last.then_inc(s_full, 1)

                def steps(g, s, n0, n1, before, between):
                    for n in range(n0, n1, 2):
                        kt, h = divmod(n, GH)
                        keys_by_queries(g, s, n)
                        between(n)
                        between(n + 1)
                        keys_by_queries(g, s, n + 1)
                        if kt:
                            weigh(g, s, kt - 1, h // 2)
                        elif before is not None:
                            weigh(*before, ST - 1, h // 2)

                def body(g, k, i, units):
                    where = {unit: n for n, unit in enumerate(units)}
                    sets = {"score": (k + 1) % SETS, "next": (k + 2) % SETS}

                    def between(inner):
                        def make(n):
                            for unit in units_of(n, inner):
                                if unit not in where:
                                    continue
                                kind, u = unit
                                number, ps = START + g * RG + where[unit], slot(START + where[unit])
                                if kind == "max":
                                    turn_max(sets["score"], number, ps, START + g * RG + where["score", SCORES - 1] + 1)
                                elif kind == "out":
                                    turn_out(g, number, ps)
                                else:
                                    if kind == "next" and u == 0:
                                        pe.wait_ge(loaded[sets[kind]], 16 * LOADS * (i + (k + 2) // SETS + 1))
                                    score(sets[kind], u, number, ps)
                        return make

                    steps(g, k, TURN, STEPS, None, between(True))
                    steps(g + 1, (k + 1) % SETS, 0, TURN, (g, k), between(False))

                def first_between(n):
                    u = n + LEAD
                    score(1, u, SCORES + 1 + u, slot(SCORES + 1 + u))

                pe.wait_ge(ones_set, SETS)
                pe.wait_ge(loaded[0], 16 * LOADS)
                for u in range(SCORES):
                    score(0, u, u, slot(u))
                turn_max(0, SCORES, slot(SCORES), SCORES)
                pe.wait_ge(loaded[1], 16 * LOADS)
                for u in range(LEAD):
                    score(1, u, SCORES + 1 + u, slot(SCORES + 1 + u))
                steps(0, 0, 0, TURN, None, first_between)
                with pe.Fori(0, (GROUPS - SETS) // SETS) as i:
                    for k in range(SETS):
                        body(i * SETS + k, k, i, in_body)
                for g in range((GROUPS - SETS) // SETS * SETS, GROUPS - 1):
                    body(g, g % SETS, g // SETS, in_last if g == GROUPS - 2 else in_body)
                g, k = GROUPS - 1, (GROUPS - 1) % SETS
                steps(g, k, TURN, STEPS, None, lambda n: None)
                for c in range(HALVES):
                    weigh(g, k, ST - 1, c)
                turn_out(g, END, slot(END))


def load_attention(sp, scr, b, h, att, loaded):
    for hg in range(NG):
        sp.dma_start(att[:, :, hg * GD:(hg + 1) * GD],
                     scr[bass.ds(b * NG + hg, 1), h * CH:(h + 1) * CH, :].rearrange("o (t p) c -> p (o t) c", p=P)).then_inc(loaded, 16)


def tile_of(x, n):
    return x[:, bass.ds(n, 1), :].rearrange("p o c -> p (o c)")


def project_ffn(p):
    nc, a = p.nc, p.a
    with ExitStack() as ctx:
        def sb(name, shape, dt=F32):
            return p.sb("f_" + name, shape, dt, ctx)

        def sem(name):
            return p.sem("f_" + name)

        w = {n: sb(f"w_{n}", [P, KC, D]) for n in ("out", "q2", "k2", "v2")}
        ln1, obias = sb("ln1", [P, KC]), sb("obias", [P, D])
        att = [sb(f"att{h}", [P, CT, D]) for h in range(2)]
        attT = [sb(f"attT{h}", [P, KC, CH]) for h in range(2)]
        y = [sb(f"y{h}", [P, CT, D]) for h in range(2)]
        yn = [sb(f"yn{h}", [P, CT, D]) for h in range(2)]
        u = [sb(f"u{h}", [P, CT, D]) for h in range(2)]
        z = [sb(f"z{h}", [P, CT, D]) for h in range(2)]
        zT = [sb(f"zT{h}", [P, KC, CH]) for h in range(2)]
        square = sb("square", [P, CT, D])
        stats = [[sb(f"stats{j}{h}", [P, CT, 6]) for h in range(2)] for j in range(2)]
        mv = [[sb(f"mv{j}{h}", [P, CT, 2]) for h in range(2)] for j in range(2)]
        ssum = [sb(f"ssum{h}", [P, CT]) for h in range(2)]
        sd = [[sb(f"sd{j}{h}", [P, CT]) for h in range(2)] for j in range(3)]
        rstd = [[sb(f"rstd{j}{h}", [P, CT]) for h in range(2)] for j in range(3)]
        rest = [sb(f"rest{k}", [P, CH]) for k in range(2)]
        parts = [sb(f"parts{k}", [P, PARTS, CH], BF16) for k in range(2)]
        vout = [sb(f"v{h}", [P, CT, H, VW]) for h in range(2)]
        t_ps = p.ps("f_t_ps", [P, KC, CH], ctx)
        y_ps = p.ps("f_y_ps", [P, CT, D], ctx)
        v_ps = p.ps("f_v_ps", [P, CT, D], ctx)
        unit_ps = [p.ps(f"f_unit_ps{k}", [P, CH], ctx) for k in range(2)]

        w_in, w_scaled, v_ones = sem("w_in"), sem("w_scaled"), sem("v_ones")
        att_in = [sem(f"att_in{h}") for h in range(2)]
        t_done, tT_done = sem("t_done"), sem("tT_done")
        yps_done, y_done, yn_done, x1_done = sem("yps_done"), sem("y_done"), sem("yn_done"), sem("x1_done")
        stats_done, mv_done = [sem(f"stats_done{j}") for j in range(2)], [sem(f"mv_done{j}") for j in range(2)]
        sd_done, rstd_done = [sem(f"sd_done{j}") for j in range(3)], [sem(f"rstd_done{j}") for j in range(3)]
        u_done, square_done, z_done = sem("u_done"), sem("square_done"), sem("z_done")
        unit_done, rest_done = sem("unit_done"), sem("rest_done")
        part_done = [sem(f"part{n}_done") for n in range(PARTS)]
        v_done, v_copied = sem("v_done"), sem("v_copied")
        parts_free = [sem(f"parts_free{k}") for k in range(2)]
        vout_free = [sem(f"vout_free{h}") for h in range(2)]
        u_free = [sem(f"u_free{h}") for h in range(2)]
        zT_free = [sem(f"zT_free{h}") for h in range(2)]
        UC = 2 * KC
        UB = UC * HALVES
        N_LOADS = 6

        def chunk(b, h):
            return b * HALVES + h

        def unit(b, h, i):
            return b * UB + (h * UC + i)

        def fill(b, which, h):
            return b * 2 * HALVES + (which * HALVES + h)

        with nc.Block() as block:
            @block.sync
            def _(sp):
                def load(b, h):
                    wait_apart(p, sp, t_done, fill(b, 0, h) + 1)
                    load_attention(sp, p.att_scr[0], b, h, att[h], att_in[h])

                def stores(b, h):
                    n = chunk(b, h)
                    wait_apart(p, sp, u_done, CT * (n + 1))
                    sp.dma_start(p.u_scr[bass.ds(n * CH, CH), :].rearrange("(t p) c -> p t c", p=P), u[h][:]).then_inc(u_free[h], 16)
                    wait_apart(p, sp, tT_done, fill(b, 1, h) + 2)
                    sp.dma_start(p.zT_scr[:, bass.ds(n * CH, CH)].rearrange("(k p) t -> p k t", p=P), zT[h][:]).then_inc(zT_free[h], 16)
                    for i in range(UC):
                        m = i % KC
                        scr = (p.q_scr if i < KC else p.k_scr)[1]
                        wait_apart(p, sp, part_done[2], unit(b, h, i) + 1)
                        sp.dma_start(scr[:, bass.ds(b * D + m * P, P), h * CH:(h + 1) * CH].rearrange("a r t -> r a t"),
                                     parts[i % 2][:]).then_inc(parts_free[i % 2], 16)
                    wait_apart(p, sp, v_copied, CT * (n + 2))
                    store_v(sp, p.v_scr[1], b, h, vout[h], vout_free[h])

                for h in range(2):
                    sp.sem_inc(parts_free[h], 16)
                    sp.sem_inc(u_free[h], 16)
                    sp.sem_inc(zT_free[h], 16)
                    sp.sem_inc(vout_free[h], 16 * NG)
                load(0, 0)
                load(0, 1)
                with sp.Fori(0, B - 1) as b:
                    stores(b, 0)
                    load(b + 1, 0)
                    stores(b, 1)
                    load(b + 1, 1)
                stores(B - 1, 0)
                stores(B - 1, 1)
                for h in range(2):
                    wait_apart(p, sp, parts_free[h], 16 * (B * UB // 2 + 1))
                    wait_apart(p, sp, vout_free[h], 16 * NG * (B + 1))
                    wait_apart(p, sp, u_free[h], 16 * (B + 1))
                    wait_apart(p, sp, zT_free[h], 16 * (B + 1))

            @block.gpsimd
            def _(pool):
                for h in range(2):
                    nc.gpsimd.memset(vout[h][:], 1.0).then_inc(v_ones, 1)
                with pool.Fori(0, B) as b:
                    for h in range(HALVES):
                        for t in range(CT):
                            tile = chunk(b, h) * CT + t
                            pool.wait_ge(yn_done, tile + 1)
                            nc.gpsimd.tensor_tensor(tile_of(p.x_all, tile), tile_of(p.x_all, tile), yn[h][:, t, :], ALU.add).then_inc(x1_done, 1)
                    for h in range(HALVES):
                        for i in range(UC):
                            pool.wait_ge(part_done[1], unit(b, h, i) + 1)
                            nc.gpsimd.tensor_tensor(parts[i % 2][:, 2, :], rest[i % 2][:], parts[i % 2][:, 1, :], ALU.subtract).then_inc(part_done[2], 1)

            @block.scalar
            def _(act):
                for n in ("out", "q2", "k2", "v2"):
                    act.dma_start(w[n][:], rows_in(a["w_" + n])).then_inc(w_in, 16)
                act.dma_start(ln1[:], a["ln1"]).then_inc(w_in, 16)
                act.dma_start(obias[:], a["out_bias"]).then_inc(w_in, 16)
                act.sem_inc(tT_done, 1)

                def root(b, h, j):
                    act.wait_ge(mv_done[j], CT * (chunk(b, h) + 1))
                    nc.scalar.activation(sd[j][h][:], mv[j][h][:, :, 1], ACT.Sqrt, bias=p.eps[:, 0:1]).then_inc(sd_done[j], 1)

                with act.Fori(0, B) as b:
                    for h in range(HALVES):
                        act.wait_ge(t_done, fill(b, 0, h) + 1 + 2 * HALVES)
                        nc.scalar.copy(attT[h][:], t_ps[:]).then_inc(tT_done, 1)
                    for j in range(2):
                        for h in range(HALVES):
                            root(b, h, j)
                    for h in range(HALVES):
                        n = chunk(b, h)
                        for t in range(CT):
                            act.wait_ge(u_done, n * CT + t + 1)
                            if t:
                                act.wait_ge(square_done, n * CT + t)
                            nc.scalar.activation(square[:, t, :], u[h][:, t, :], ACT.Square, accum_out=ssum[h][:, t:t + 1]).then_inc(square_done, 1)
                        act.wait_ge(square_done, CT * (n + 1))
                        nc.scalar.activation(sd[2][h][:], ssum[h][:], ACT.Sqrt, bias=p.eps[:, 1:2], scale=1.0 / D).then_inc(sd_done[2], 1)
                    for h in range(HALVES):
                        act.wait_ge(zT_free[h], 16 * (b + 1))
                        act.wait_ge(t_done, fill(b, 1, h) + 1 + 2 * HALVES)
                        nc.scalar.copy(zT[h][:], t_ps[:]).then_inc(tT_done, 1)
                        for i in range(UC):
                            k, n = i % 2, unit(b, h, i)
                            act.wait_ge(parts_free[k], 16 * (b * (UB // 2) + h * (UC // 2) + i // 2 + 1))
                            act.wait_ge(unit_done, n + 1)
                            nc.scalar.copy(parts[k][:, 0, :], unit_ps[k][:]).then_inc(part_done[0], 1)
                            act.wait_ge(rest_done, n + 1 + AHEAD)
                            nc.scalar.copy(parts[k][:, 1, :], rest[k][:]).then_inc(part_done[1], 1)

            @block.vector
            def _(dve):
                def moments(b, h, j, src, ready):
                    n = chunk(b, h)
                    for t in range(CT):
                        dve.wait_ge(ready, n * CT + t + 1)
                        nc.vector.bn_stats(stats[j][h][:, t, :], src(n * CT + t, t)).then_inc(stats_done[j], 1)
                    wait_apart(p, dve, stats_done[j], CT * (n + 1))
                    for t in range(CT):
                        nc.vector.bn_aggr(mv[j][h][:, t, :], stats[j][h][:, t, :]).then_inc(mv_done[j], 1)

                def invert(b, h, j):
                    n = chunk(b, h)
                    dve.wait_ge(sd_done[j], n + 1)
                    nc.vector.reciprocal(rstd[j][h][:], sd[j][h][:]).then_inc(rstd_done[j], 1)
                    dve.wait_ge(rstd_done[j], n + 1)

                dve.sem_inc(v_copied, CT)
                dve.sem_inc(y_done, CT)
                dve.sem_inc(rest_done, AHEAD)
                dve.wait_ge(v_ones, 2)
                dve.wait_ge(w_in, 16 * N_LOADS)
                for name in ("q2", "k2", "v2"):
                    for kc in range(KC):
                        nc.vector.tensor_scalar(w[name][:, kc, :], w[name][:, kc, :], ln1[:, kc:kc + 1], None, ALU.mult).then_inc(w_scaled, 1)
                with dve.Fori(0, B) as b:
                    for h in range(HALVES):
                        n = chunk(b, h)
                        dve.wait_ge(yps_done, n + 1)
                        for t in range(CT):
                            nc.vector.tensor_tensor(y[h][:, t, :], y_ps[:, t, :], obias[:], ALU.add).then_inc(y_done, 1)
                    for h in range(HALVES):
                        n = chunk(b, h)
                        dve.wait_ge(y_done, CT * (n + 2))
                        moments(b, h, 0, lambda tile, t: y[h][:, t, :], y_done)
                    for h in range(HALVES):
                        invert(b, h, 0)
                        for t in range(CT):
                            nc.vector.tensor_scalar(yn[h][:, t, :], y[h][:, t, :], mv[0][h][:, t, 0:1], rstd[0][h][:, t:t + 1],
                                                    ALU.subtract, ALU.mult).then_inc(yn_done, 1)
                    for h in range(HALVES):
                        moments(b, h, 1, lambda tile, t: tile_of(p.x_all, tile), x1_done)
                    for h in range(HALVES):
                        invert(b, h, 1)
                        dve.wait_ge(u_free[h], 16 * (b + 1))
                        for t in range(CT):
                            nc.vector.tensor_scalar(u[h][:, t, :], tile_of(p.x_all, chunk(b, h) * CT + t), mv[1][h][:, t, 0:1],
                                                    rstd[1][h][:, t:t + 1], ALU.subtract, ALU.mult).then_inc(u_done, 1)
                    for h in range(HALVES):
                        invert(b, h, 2)
                        for t in range(CT):
                            nc.vector.tensor_scalar(z[h][:, t, :], u[h][:, t, :], rstd[2][h][:, t:t + 1], None, ALU.mult).then_inc(z_done, 1)
                    for h in range(HALVES):
                        dve.wait_ge(v_done, chunk(b, h) + 1)
                        dve.wait_ge(vout_free[h], 16 * NG * (b + 1))
                        for t in range(CT):
                            nc.vector.tensor_copy(vout[h][:, t, :, 0:HD], v_ps[:, t, :].rearrange("p (h c) -> p h c", c=HD)).then_inc(v_copied, 1)
                        for i in range(UC):
                            k, n = i % 2, unit(b, h, i)
                            dve.wait_ge(part_done[0], n + 1)
                            nc.vector.tensor_tensor(rest[k][:], unit_ps[k][:], parts[k][:, 0, :], ALU.subtract).then_inc(rest_done, 1)

            @block.tensor
            def _(pe):
                def turn(b, which, h, src, ready):
                    pe.wait_ge(ready, 16 * NG * (b + 1) if which == 0 else CT * (chunk(b, h) + 1))
                    pe.wait_ge(tT_done, fill(b, which, h) + 1)
                    for kc in range(KC):
                        for t in range(CT):
                            last = nc.tensor.transpose(t_ps[:, kc, t * P:(t + 1) * P], src[:, t, kc * P:(kc + 1) * P], p.ident[:])
                    last.then_inc(t_done, 1)
                    pe.wait_ge(tT_done, fill(b, which, h) + 2)

                def by_tokens(ps, srcT, weight, done):
                    for t in range(CT):
                        for kc in range(KC):
                            last = nc.tensor.matmul(ps[:, t, :], srcT[:, kc, t * P:(t + 1) * P], weight[:, kc, :],
                                                    start=kc == 0, stop=kc == KC - 1)
                    last.then_inc(done, 1)

                pe.sem_inc(t_done, 2 * HALVES)
                pe.wait_ge(w_in, 16 * N_LOADS)
                pe.wait_ge(w_scaled, 3 * KC)
                with pe.Fori(0, B) as b:
                    for h in range(HALVES):
                        turn(b, 0, h, att[h], att_in[h])
                        pe.wait_ge(y_done, CT * (chunk(b, h) + 1))
                        by_tokens(y_ps, attT[h], w["out"], yps_done)
                    for h in range(HALVES):
                        turn(b, 1, h, z[h], z_done)
                        pe.wait_ge(v_copied, CT * (chunk(b, h) + 1))
                        by_tokens(v_ps, zT[h], w["v2"], v_done)
                        for i in range(UC):
                            m, name = i % KC, ("q2" if i < KC else "k2")
                            pe.wait_ge(rest_done, unit(b, h, i) + 1)
                            for kc in range(KC):
                                last = nc.tensor.matmul(unit_ps[i % 2][:], w[name][:, kc, m * P:(m + 1) * P], zT[h][:, kc, :],
                                                        start=kc == 0, stop=kc == KC - 1)
                            last.then_inc(unit_done, 1)


def feed_forward(p):
    nc, a = p.nc, p.a
    with ExitStack() as ctx:
        def sb(name, shape, dt=F32):
            return p.sb("g_" + name, shape, dt, ctx)

        def sem(name):
            return p.sem("g_" + name)

        w_gate, w_up = sb("w_gate", [P, KC, F]), sb("w_up", [P, KC, F])
        w_down = sb("w_down", [P, FC, D])
        w_o = sb("w_o", [P, KC, D])
        a_pad, a_ln = sb("a_pad", [P, KC, P]), sb("a_ln", [P, KC, P])
        b_pad, woa = sb("b_pad", [P, F]), sb("woa", [P, KC, P])
        ln2 = sb("ln2", [P, KC])
        att = [sb(f"att{h}", [P, CT, D]) for h in range(2)]
        attT = sb("attT", [P, KC, CH])
        zT = [sb(f"zT{h}", [P, KC, CH]) for h in range(2)]
        u = [sb(f"u{h}", [P, CT, D]) for h in range(2)]
        mod = sb("mod", [P, CH])
        modh = [sb(f"modh{h}", [P, CH]) for h in range(2)]
        silu = [sb(f"silu{j}", [P, CH]) for j in range(2)]
        hidden = sb("hidden", [P, FC, CH])
        m = sb("m", [P, CT, D])
        mn = sb("mn", [P, CT, D])
        result = [sb(f"result{h}", [P, CT, D]) for h in range(2)]
        stats, mv = sb("stats", [P, CT, 6]), sb("mv", [P, CT, 2])
        sd, rstd = sb("sd", [P, CT]), sb("rstd", [P, CT])
        t_ps = p.ps("g_t_ps", [P, KC, CH], ctx)
        gate_ps = [p.ps(f"g_gate_ps{j}", [P, CH], ctx) for j in range(2)]
        up_ps = [p.ps(f"g_up_ps{j}", [P, CH], ctx) for j in range(2)]
        down_ps = p.ps("g_down_ps", [P, CT, D], ctx)

        w_in, zeroed, w_scaled, woa_made, woa_done = (sem(n) for n in ("w_in", "zeroed", "w_scaled", "woa_made", "woa_done"))
        chunk_in = [sem(f"chunk_in{h}") for h in range(2)]
        t_done, attT_done, low_done, mod_done, modh_done = (sem(n) for n in ("t_done", "attT_done", "low_done", "mod_done", "modh_done"))
        gate_done, up_done, silu_done, hidden_done = (sem(n) for n in ("gate_done", "up_done", "silu_done", "hidden_done"))
        down_done, m_done, stats_done, mv_done, sd_done, rstd_done, mn_done, result_done = (
            sem(n) for n in ("down_done", "m_done", "stats_done", "mv_done", "sd_done", "rstd_done", "mn_done", "result_done"))
        result_free = [sem(f"result_free{h}") for h in range(2)]
        N_LOADS = 4 + 1 + 1 + 1
        C_LOADS = NG + 2

        def chunk(b, h):
            return b * HALVES + h

        with nc.Block() as block:
            @block.sync
            def _(sp):
                def load(b, h):
                    n = chunk(b, h)
                    wait_apart(p, sp, mn_done, CT * (n + 1))
                    load_attention(sp, p.att_scr[1], b, h, att[h], chunk_in[h])
                    sp.dma_start(zT[h][:], p.zT_scr[:, bass.ds(n * CH, CH)].rearrange("(k p) t -> p k t", p=P)).then_inc(chunk_in[h], 16)
                    sp.dma_start(u[h][:], p.u_scr[bass.ds(n * CH, CH), :].rearrange("(t p) c -> p t c", p=P)).then_inc(chunk_in[h], 16)

                def store(b, h):
                    n = chunk(b, h)
                    wait_apart(p, sp, result_done, CT * (n + 2))
                    sp.dma_start(p.out[bass.ds(n * CH, CH), :].rearrange("(t p) c -> p t c", p=P), result[h][:]).then_inc(result_free[h], 16)

                for h in range(2):
                    sp.sem_inc(result_free[h], 16)
                load(0, 0)
                load(0, 1)
                with sp.Fori(0, B - 1) as b:
                    for h in range(HALVES):
                        store(b, h)
                        load(b + 1, h)
                store(B - 1, 0)
                store(B - 1, 1)
                for h in range(2):
                    wait_apart(p, sp, result_free[h], 16 * (B + 1))

            @block.gpsimd
            def _(pool):
                nc.gpsimd.memset(a_pad[:], 0.0).then_inc(zeroed, 1)
                nc.gpsimd.memset(b_pad[:], 0.0).then_inc(zeroed, 1)
                pool.sem_inc(result_done, CT)
                with pool.Fori(0, B) as b:
                    for h in range(HALVES):
                        pool.wait_ge(result_free[h], 16 * (b + 1))
                        for t in range(CT):
                            tile = chunk(b, h) * CT + t
                            pool.wait_ge(mn_done, 2 * CT + tile + 1)
                            nc.gpsimd.tensor_tensor(result[h][:, t, :], tile_of(p.x_all, tile), mn[:, t, :], ALU.add).then_inc(result_done, 1)

            @block.scalar
            def _(act):
                for t, n in ((w_gate, "w_gate"), (w_up, "w_up"), (w_down, "w_down"), (w_o, "w_o")):
                    act.dma_start(t[:], rows_in(a[n])).then_inc(w_in, 16)
                act.dma_start(ln2[:], a["ln2"]).then_inc(w_in, 16)
                act.wait_ge(zeroed, 2)
                act.dma_start(a_pad[:, :, 0:R], rows_in(a["a"])).then_inc(w_in, 16)
                act.dma_start(b_pad[0:R, :], a["b"]).then_inc(w_in, 16)
                act.wait_ge(woa_made, 1)
                nc.scalar.copy(woa[:], t_ps[:, :, 0:P]).then_inc(woa_done, 1)

                def low_rank(b, h):
                    n = chunk(b, h)
                    act.wait_ge(t_done, n + 1)
                    nc.scalar.copy(attT[:], t_ps[:]).then_inc(attT_done, 1)
                    act.wait_ge(low_done, n + 1)
                    act.wait_ge(modh_done, n + 1)
                    nc.scalar.activation(mod[:], t_ps[:, 0, :], ACT.Tanh).then_inc(mod_done, 1)

                def gates(b, h):
                    for f in range(FC):
                        n = chunk(b, h) * FC + f
                        act.wait_ge(gate_done, n + 1)
                        act.wait_ge(hidden_done, n + 1)
                        nc.scalar.activation(silu[f % 2][:], gate_ps[f % 2][:], ACT.Silu).then_inc(silu_done, 1)

                def root(b, h):
                    act.wait_ge(mv_done, CT * (chunk(b, h) + 1))
                    nc.scalar.activation(sd[:], mv[:, :, 1], ACT.Sqrt, bias=p.eps[:, 0:1]).then_inc(sd_done, 1)

                with act.Fori(0, B) as b:
                    low_rank(b, 0)
                    gates(b, 0)
                    low_rank(b, 1)
                    root(b, 0)
                    gates(b, 1)
                    root(b, 1)

            @block.vector
            def _(dve):
                dve.sem_inc(modh_done, 1)
                dve.sem_inc(hidden_done, AHEAD)
                dve.sem_inc(m_done, CT)
                dve.sem_inc(mn_done, 2 * CT)
                dve.wait_ge(w_in, 16 * N_LOADS)
                for kc in range(KC):
                    nc.vector.tensor_scalar(w_gate[:, kc, :], w_gate[:, kc, :], ln2[:, kc:kc + 1], None, ALU.mult).then_inc(w_scaled, 1)
                    nc.vector.tensor_scalar(w_up[:, kc, :], w_up[:, kc, :], ln2[:, kc:kc + 1], None, ALU.mult).then_inc(w_scaled, 1)
                    nc.vector.tensor_scalar(a_ln[:, kc, :], a_pad[:, kc, :], ln2[:, kc:kc + 1], None, ALU.mult).then_inc(w_scaled, 1)

                def low_rank(b, h):
                    n = chunk(b, h)
                    dve.wait_ge(mod_done, n + 1)
                    nc.vector.scalar_tensor_tensor(modh[h][:], mod[:], MOD_SCALE, t_ps[:, 1, :], ALU.mult, ALU.mult).then_inc(modh_done, 1)

                def gates(b, h):
                    for f in range(FC):
                        n = chunk(b, h) * FC + f
                        dve.wait_ge(up_done, n + 1)
                        dve.wait_ge(silu_done, n + 1)
                        nc.vector.tensor_tensor(hidden[:, f, :], silu[f % 2][:], up_ps[f % 2][:], ALU.mult).then_inc(hidden_done, 1)

                def finish(b, h):
                    n = chunk(b, h)
                    dve.wait_ge(down_done, n + 1)
                    for t in range(CT):
                        nc.vector.tensor_tensor(m[:, t, :], down_ps[:, t, :], u[h][:, t, :], ALU.add).then_inc(m_done, 1)
                    for t in range(CT):
                        dve.wait_ge(m_done, CT * (n + 1) + t + 1)
                        nc.vector.bn_stats(stats[:, t, :], m[:, t, :]).then_inc(stats_done, 1)
                    wait_apart(p, dve, stats_done, CT * (n + 1))
                    for t in range(CT):
                        nc.vector.bn_aggr(mv[:, t, :], stats[:, t, :]).then_inc(mv_done, 1)
                    dve.wait_ge(sd_done, n + 1)
                    nc.vector.reciprocal(rstd[:], sd[:]).then_inc(rstd_done, 1)
                    dve.wait_ge(rstd_done, n + 1)
                    dve.wait_ge(result_done, CT * (n + 1))
                    for t in range(CT):
                        nc.vector.tensor_scalar(mn[:, t, :], m[:, t, :], mv[:, t, 0:1], rstd[:, t:t + 1], ALU.subtract, ALU.mult).then_inc(mn_done, 1)

                with dve.Fori(0, B) as b:
                    low_rank(b, 0)
                    gates(b, 0)
                    low_rank(b, 1)
                    finish(b, 0)
                    gates(b, 1)
                    finish(b, 1)

            @block.tensor
            def _(pe):
                def low_rank(b, h):
                    n = chunk(b, h)
                    pe.wait_ge(chunk_in[h], 16 * C_LOADS * (b + 1))
                    pe.wait_ge(modh_done, n + 1)
                    for kc in range(KC):
                        for t in range(CT):
                            last = nc.tensor.transpose(t_ps[:, kc, t * P:(t + 1) * P], att[h][:, t, kc * P:(kc + 1) * P], p.ident[:])
                    last.then_inc(t_done, 1)
                    pe.wait_ge(attT_done, n + 1)
                    for j, (weight, src) in enumerate(((woa, attT), (a_ln, zT[h]))):
                        for kc in range(KC):
                            last = nc.tensor.matmul(t_ps[:, j, :], weight[:, kc, :], src[:, kc, :], start=kc == 0, stop=kc == KC - 1)
                    last.then_inc(low_done, 1)

                def gates(b, h):
                    pe.wait_ge(modh_done, chunk(b, h) + 2)
                    for f in range(FC):
                        n, cols = chunk(b, h) * FC + f, slice(f * P, (f + 1) * P)
                        pe.wait_ge(hidden_done, n + 1)
                        for kc in range(KC):
                            nc.tensor.matmul(gate_ps[f % 2][:], w_gate[:, kc, cols], zT[h][:, kc, :], start=kc == 0, stop=False)
                        nc.tensor.matmul(gate_ps[f % 2][:], b_pad[:, cols], modh[h][:], start=False, stop=True).then_inc(gate_done, 1)
                        for kc in range(KC):
                            last = nc.tensor.matmul(up_ps[f % 2][:], w_up[:, kc, cols], zT[h][:, kc, :], start=kc == 0, stop=kc == KC - 1)
                        last.then_inc(up_done, 1)

                def down(b, h):
                    n = chunk(b, h)
                    pe.wait_ge(hidden_done, FC * (n + 1) + AHEAD)
                    pe.wait_ge(m_done, CT * (n + 1))
                    for t in range(CT):
                        for f in range(FC):
                            last = nc.tensor.matmul(down_ps[:, t, :], hidden[:, f, t * P:(t + 1) * P], w_down[:, f, :],
                                                    start=f == 0, stop=f == FC - 1)
                    last.then_inc(down_done, 1)

                pe.wait_ge(w_in, 16 * N_LOADS)
                for kc in range(KC):
                    for ko in range(KC):
                        last = nc.tensor.matmul(t_ps[:, kc, 0:P], w_o[:, ko, kc * P:(kc + 1) * P], a_pad[:, ko, :],
                                                start=ko == 0, stop=ko == KC - 1)
                last.then_inc(woa_made, 1)
                pe.wait_ge(woa_done, 1)
                pe.wait_ge(w_scaled, 3 * KC)
                with pe.Fori(0, B) as b:
                    low_rank(b, 0)
                    gates(b, 0)
                    low_rank(b, 1)
                    down(b, 0)
                    gates(b, 1)
                    down(b, 1)


def constant_arrays():
    half = HD // 2
    inv_freq = (1.0 / np.float32(10000.0) ** (np.arange(0, HD, 2, dtype=np.float32) / np.float32(HD))).astype(np.float32)
    freqs = np.arange(S, dtype=np.float32)[None, :] * inv_freq[:, None]
    rows = np.arange(P) % half
    sign = np.where(np.arange(P) % HD < half, np.float32(-1), np.float32(1))[:, None]
    cos = np.cos(freqs)[rows].astype(np.float32)
    sin = (np.sin(freqs)[rows] * sign).astype(np.float32)
    turned = np.arange(D) // HD * HD + (np.arange(D) % HD + half) % HD
    return cos, sin, turned


def kernel(**inputs):
    from concourse import bacc
    from concourse.bass_utils import run_bass_kernel_spmd

    def attn(n):
        return np.asarray(inputs["L0_attn_" + n])

    def ffn(n):
        return np.asarray(inputs["L0_ffn_" + n])

    def by_partition(v):
        return v.reshape(KC, P).T

    cos, sin, turned = constant_arrays()
    data = {
        "x": attn("x").reshape(B * S, D),
        "w_q": attn("q_w").T, "w_qr": attn("q_w")[turned].T,
        "w_k": attn("k_w").T, "w_kr": attn("k_w")[turned].T,
        "w_v": attn("v_w").T, "w_out": attn("out_w").T,
        "qk_bias": np.stack([by_partition(v) for v in (attn("q_b"), attn("q_b")[turned], attn("k_b"), attn("k_b")[turned])], axis=1),
        "v_bias": np.broadcast_to(attn("v_b"), (P, D)), "out_bias": np.broadcast_to(attn("out_b"), (P, D)),
        "cos": cos, "sin": sin,
        "ln1": by_partition(ffn("ln1_w")), "ln2": by_partition(ffn("ln2_w")),
        "w_q2": ffn("Wq").T, "w_k2": ffn("Wk").T, "w_v2": ffn("Wv").T, "w_o": ffn("Wo"),
        "a": ffn("A"), "b": ffn("B"),
        "w_gate": ffn("W_in_base").T, "w_up": ffn("W_up_base").T, "w_down": ffn("W_down").T,
    }
    nc = bacc.Bacc("TRN2", target_bir_lowering=False, num_devices=1)
    arrays, args = {}, {}
    for name, value in data.items():
        value = np.ascontiguousarray(value)
        arrays["in_" + name] = value
        args[name] = nc.dram_tensor("in_" + name, value.shape, mybir.dt.from_np(value.dtype), kind="ExternalInput").ap()
    out = nc.dram_tensor("out_x", (B * S, D), F32, kind="ExternalOutput").ap()
    build(nc, args, out)
    r = run_bass_kernel_spmd(nc, [arrays], core_ids=[0])
    return r.results[0]["out_x"].reshape(B, S, D)
```

```python
from contextlib import ExitStack

import numpy as np

import concourse.bass as bass
from concourse import mybir

F32 = mybir.dt.float32
BF16 = mybir.dt.bfloat16
F32R = mybir.dt.float32r
ALU = mybir.AluOpType
ACT = mybir.ActivationFunctionType
AX = mybir.AxisListType

P = 128
B, S, D = 4, 1024, 256
H, HD = 16, 16
F = 1024
R = 16
KC = D // P
FC = F // P
CH = 512
CT = CH // P
HALVES = S // CH
GH = 4
GROUPS = B * H // GH
GD = GH * HD
NG = H // GH
ST = S // P
VW = 32
PARTS = 3
Q_PARTS = [0, 0, 1, 1, 0, 2]
K_PARTS = [0, 1, 0, 1, 2, 0]
SROWS = HD * len(Q_PARTS)
AROWS = SROWS + 2
SETS = 3
SCALE = HD ** -0.5
REPS = P // R
MOD_PARTS = [0, 1, 0, 2]
B_PARTS = [0, 1, 0, 1, 2, None, 0, None]
Q1, Q3 = slice(P // 4, P // 2), slice(3 * P // 4, P)
AHEAD = 2
LN_EPS, RMS_EPS = 1e-5, 1e-6
MOD_SCALE = 0.1
MASKED = -1e30


class Program:

    def __init__(self, nc, ctx, a, out):
        self.nc, self.ctx, self.a, self.out = nc, ctx, a, out

    def sb(self, name, shape, dt=F32, ctx=None):
        return (ctx or self.ctx).enter_context(self.nc.sbuf_tensor(name, shape, dt))

    def ps(self, name, shape, ctx, dt=F32):
        return ctx.enter_context(self.nc.psum_tensor(name, shape, dt))

    def sem(self, name):
        return self.ctx.enter_context(self.nc.semaphore(name))


def build(nc, a, out):
    with ExitStack() as ctx:
        p = Program(nc, ctx, a, out)
        p.q_scr = [nc.dram_tensor(f"q_scr{n}", (PARTS, B * D, S), BF16, kind="Internal").ap() for n in range(2)]
        p.k_scr = [nc.dram_tensor(f"k_scr{n}", (PARTS, B * D, S), BF16, kind="Internal").ap() for n in range(2)]
        p.v_scr = [nc.dram_tensor(f"v_scr{n}", (GROUPS, S, GH * VW), F32, kind="Internal").ap() for n in range(2)]
        p.att_scr = [nc.dram_tensor(f"att_scr{n}", (GROUPS, S, GD), F32, kind="Internal").ap() for n in range(2)]
        p.u_scr = nc.dram_tensor("u_scr", (B * S, D), F32, kind="Internal").ap()
        p.zT_scr = nc.dram_tensor("zT_scr", (D, B * S), F32, kind="Internal").ap()
        p.ident = p.sb("ident", [P, P])
        p.ident_bf = p.sb("ident_bf", [P, P], BF16)
        p.causal = p.sb("causal", [P, 2, P], BF16)
        p.eps = p.sb("eps", [P, 2])
        p.x_all = p.sb("x_all", [P, B * ST, D])
        p.waits_apart = p.sem("waits_apart")
        constants(p)
        project_rope(p)
        attention(p, 0, causal=False)
        project_ffn(p)
        with ExitStack() as lasting:
            with ExitStack() as passing:
                weights = FfnWeights(p, lasting, passing)
                attention(p, 1, causal=True, behind=weights)
            feed_forward(p, weights)


def constants(p):
    nc = p.nc
    x_rows = [(h * CH, (h + 1) * CH) for h in range(HALVES)] + [(b * S, (b + 1) * S) for b in range(1, B)]
    p.x_in = [p.sem(f"x_in{n}") for n in range(len(x_rows))]
    zeroed, shaped = p.sem("const_zeroed"), p.sem("constants_shaped")
    with nc.Block() as block:
        @block.sync
        def _(sp):
            for n, (lo, hi) in enumerate(x_rows):
                sp.dma_start(p.x_all[:, lo // P:hi // P, :], p.a["x"][lo:hi, :].rearrange("(t p) c -> p t c", p=P)).then_inc(p.x_in[n], 16)

        @block.gpsimd
        def _(pool):
            nc.gpsimd.memset(p.ident[:], 0.0).then_inc(zeroed, 1)
            nc.gpsimd.memset(p.ident_bf[:], 0.0).then_inc(zeroed, 1)
            nc.gpsimd.memset(p.causal[:], 0.0).then_inc(zeroed, 1)
            nc.gpsimd.memset(p.eps[:, 0:1], LN_EPS).then_inc(zeroed, 1)
            nc.gpsimd.memset(p.eps[:, 1:2], RMS_EPS).then_inc(zeroed, 1)
            pool.wait_ge(zeroed, 5)
            for m in (p.ident, p.ident_bf):
                nc.gpsimd.affine_select(out=m[:], in_=m[:], compare_op=ALU.not_equal, fill=1.0, base=0,
                                        pattern=[[-1, P]], channel_multiplier=1).then_inc(shaped, 1)
            for form, step in ((0, -1), (1, 1)):
                nc.gpsimd.affine_select(out=p.causal[:, form, :], in_=p.causal[:, form, :], compare_op=ALU.is_ge, fill=MASKED, base=0,
                                        pattern=[[step, P]], channel_multiplier=-step).then_inc(shaped, 1)
            pool.wait_ge(shaped, 4)


def wait_apart(p, eng, sem, value):
    eng.wait_ge(sem, value)
    eng.sem_inc(p.waits_apart, 1)


def rows_in(w):
    return w.rearrange("(k p) n -> p k n", p=P)


def store_v(sp, scr, b, h, vout, stored):
    for hg in range(NG):
        sp.dma_start(scr[bass.ds(b * NG + hg, 1), h * CH:(h + 1) * CH, :].rearrange("o (t p) c -> p (o t) c", p=P),
                     vout[:, :, hg * GH:(hg + 1) * GH, :].rearrange("p t h c -> p t (h c)")).then_inc(stored, 16)


def project_rope(p):
    nc, a = p.nc, p.a
    with ExitStack() as ctx:
        def sb(name, shape, dt=F32):
            return p.sb("r_" + name, shape, dt, ctx)

        def sem(name):
            return p.sem("r_" + name)

        NAMES = ("v", "q", "qr", "k", "kr")
        w = sb("w", [P, len(NAMES), KC, D])
        w_half = [sb(f"w_{n}", [P, len(NAMES), KC, D], F32R) for n in ("hi", "lo")]
        bias = sb("bias", [P, 4, KC])
        vbias = sb("vbias", [P, D])
        cos, sin = sb("cos", [P, S]), sb("sin", [P, S])
        stats = [sb(f"stats{h}", [P, CT, 6]) for h in range(2)]
        mv = [sb(f"mv{h}", [P, CT, 2]) for h in range(2)]
        sd = [sb(f"sd{h}", [P, CT]) for h in range(2)]
        rstd = [sb(f"rstd{h}", [P, CT]) for h in range(2)]
        xn = [sb(f"xn{h}", [P, CT, D]) for h in range(2)]
        xnT = [[sb(f"xnT_{n}{h}", [P, KC, CH], F32R) for n in ("hi", "lo")] for h in range(2)]
        t_cos = [sb(f"tcos{u}", [P, CH]) for u in range(2)]
        t_sin = [sb(f"tsin{u}", [P, CH]) for u in range(2)]
        t_sum = [sb(f"tsum{u}", [P, CH]) for u in range(2)]
        rest = [sb(f"rest{u}", [P, CH]) for u in range(2)]
        parts = [sb(f"parts{u}", [P, PARTS, CH], BF16) for u in range(2 * KC)]
        vout = [sb(f"v{h}", [P, CT, H, VW]) for h in range(2)]
        t_ps = p.ps("r_t_ps", [P, KC, CH], ctx)
        pair_ps = [p.ps(f"r_pair_ps{u}", [P, 2, CH], ctx) for u in range(2)]
        v_ps = p.ps("r_v_ps", [P, CT, D], ctx)

        w_in, hi_made, lo_made = sem("w_in"), sem("w_hi_made"), sem("w_lo_made")
        stats_done, mv_done, sd_done, rstd_done, xn_done = (sem(n) for n in ("stats_done", "mv_done", "sd_done", "rstd_done", "xn_done"))
        t_done, hi_done, lo_done, pair_done = sem("t_done"), sem("hi_done"), sem("lo_done"), sem("pair_done")
        cos_done, sin_done, sum_done, rest_done = sem("cos_done"), sem("sin_done"), sem("sum_done"), sem("rest_done")
        part_done = [sem(f"part{n}_done") for n in range(PARTS)]
        v_done, v_copied, v_ones = sem("v_done"), sem("v_copied"), sem("v_ones")
        parts_free = [sem(f"parts_free{u}") for u in range(2 * KC)]
        vout_free = [sem(f"vout_free{h}") for h in range(2)]
        UC = 2 * KC
        UB = UC * HALVES
        N_LOADS = 4
        HALF_PAIRS = ((0, 0), (0, 1), (1, 0))

        def chunk(b, h):
            return b * HALVES + h

        def unit(b, h, u):
            return b * UB + (h * UC + u)

        def steps(eng, step):
            with eng.Fori(0, B - 1) as b:
                step((b, 0), (b, 1), (b + 1, 0))
                step((b, 1), (b + 1, 0), (b + 1, 1))
            step((B - 1, 0), (B - 1, 1), None)
            step((B - 1, 1), None, None)

        with nc.Block() as block:
            @block.sync
            def _(sp):
                for u in range(UC):
                    sp.sem_inc(parts_free[u], 16)
                for h in range(HALVES):
                    sp.sem_inc(vout_free[h], 16 * NG)
                with sp.Fori(0, B) as b:
                    for h in range(HALVES):
                        wait_apart(p, sp, v_copied, chunk(b, h) + 2)
                        store_v(sp, p.v_scr[0], b, h, vout[h], vout_free[h])
                        for u in range(UC):
                            m = u % KC
                            scr = (p.q_scr if u < KC else p.k_scr)[0]
                            wait_apart(p, sp, part_done[2], unit(b, h, u) + 1 + AHEAD)
                            sp.dma_start(scr[:, bass.ds(b * D + m * P, P), h * CH:(h + 1) * CH].rearrange("a r t -> r a t"),
                                         parts[u][:]).then_inc(parts_free[u], 16)
                for u in range(UC):
                    wait_apart(p, sp, parts_free[u], 16 * (B * HALVES + 1))
                for h in range(HALVES):
                    wait_apart(p, sp, vout_free[h], 16 * NG * (B + 1))

            @block.gpsimd
            def _(pool):
                def add(b, h, u):
                    k, n = u % 2, unit(b, h, u)
                    pool.wait_ge(cos_done, n + 1)
                    pool.wait_ge(sin_done, n + 1 + AHEAD)
                    pool.wait_ge(rest_done, n + 1)
                    nc.gpsimd.tensor_tensor(t_sum[k][:], t_cos[k][:], t_sin[k][:], ALU.add).then_inc(sum_done, 1)

                def last_part(b, h, u):
                    k = u % 2
                    pool.wait_ge(part_done[1], unit(b, h, u) + 1)
                    nc.gpsimd.tensor_tensor(parts[u][:, 2, :], rest[k][:], parts[u][:, 1, :], ALU.subtract).then_inc(part_done[2], 1)

                def step(this, turned, normed):
                    for u in range(UC):
                        add(*this, u)
                        if u:
                            last_part(*this, u - 1)
                    last_part(*this, UC - 1)

                for j in range(len(NAMES)):
                    pool.wait_ge(hi_made, j + 1)
                    nc.gpsimd.tensor_tensor(w_half[1][:, j, :, :], w[:, j, :, :], w_half[0][:, j, :, :].bitcast(F32), ALU.subtract).then_inc(lo_made, 1)
                for h in range(2):
                    nc.gpsimd.memset(vout[h][:], 1.0).then_inc(v_ones, 1)
                pool.sem_inc(sum_done, AHEAD)
                pool.sem_inc(part_done[2], AHEAD)
                steps(pool, step)

            @block.scalar
            def _(act):
                for j, n in enumerate(NAMES):
                    act.dma_start(w[:, j, :, :], rows_in(a["w_" + n])).then_inc(w_in, 16)
                for t, n in ((bias, "qk_bias"), (vbias, "v_bias"), (cos, "cos"), (sin, "sin")):
                    act.dma_start(t[:], a[n]).then_inc(w_in, 16)

                def root(b, h):
                    act.wait_ge(mv_done, CT * (chunk(b, h) + 1))
                    nc.scalar.activation(sd[h][:], mv[h][:, :, 1], ACT.Sqrt, bias=p.eps[:, 0:1]).then_inc(sd_done, 1)

                def round_turned(b, h):
                    act.wait_ge(t_done, chunk(b, h) + 1 + AHEAD)
                    nc.scalar.copy(xnT[h][0][:], t_ps[:]).then_inc(hi_done, 1)

                def first_part(b, h, u):
                    k = u % 2
                    act.wait_ge(parts_free[u], 16 * (chunk(b, h) + 1))
                    act.wait_ge(sum_done, unit(b, h, u) + 1 + AHEAD)
                    nc.scalar.copy(parts[u][:, 0, :], t_sum[k][:]).then_inc(part_done[0], 1)

                def second_part(b, h, u):
                    k = u % 2
                    act.wait_ge(rest_done, unit(b, h, u) + 1 + AHEAD)
                    nc.scalar.copy(parts[u][:, 1, :], rest[k][:]).then_inc(part_done[1], 1)

                def step(this, turned, normed):
                    if normed:
                        root(*normed)
                    for u in range(UC):
                        if u == 2 and turned:
                            round_turned(*turned)
                        first_part(*this, u)
                        if u:
                            second_part(*this, u - 1)
                    second_part(*this, UC - 1)

                root(0, 0)
                root(0, 1)
                act.wait_ge(w_in, 16 * (N_LOADS + len(NAMES)))
                for j in range(len(NAMES)):
                    nc.scalar.copy(w_half[0][:, j, :, :], w[:, j, :, :]).then_inc(hi_made, 1)
                round_turned(0, 0)
                steps(act, step)

            @block.vector
            def _(dve):
                def moments(b, h):
                    n = chunk(b, h)
                    for t in range(CT):
                        nc.vector.bn_stats(stats[h][:, t, :], tile_of(p.x_all, n * CT + t)).then_inc(stats_done, 1)
                    wait_apart(p, dve, stats_done, CT * (n + 1))
                    for t in range(CT):
                        nc.vector.bn_aggr(mv[h][:, t, :], stats[h][:, t, :]).then_inc(mv_done, 1)

                def normalize(b, h):
                    n = chunk(b, h)
                    dve.wait_ge(sd_done, n + 1)
                    nc.vector.reciprocal(rstd[h][:], sd[h][:]).then_inc(rstd_done, 1)
                    dve.wait_ge(rstd_done, n + 1)
                    dve.wait_ge(t_done, n + 1)
                    for t in range(CT):
                        nc.vector.tensor_scalar(xn[h][:, t, :], tile_of(p.x_all, n * CT + t),
                                                mv[h][:, t, 0:1], rstd[h][:, t:t + 1], ALU.subtract, ALU.mult).then_inc(xn_done, 1)

                def rest_turned(b, h):
                    dve.wait_ge(hi_done, chunk(b, h) + 1)
                    nc.vector.tensor_tensor(xnT[h][1][:], t_ps[:], xnT[h][0][:].bitcast(F32), ALU.subtract).then_inc(lo_done, 1)

                def turn_by_angle(b, h, u):
                    cols = slice(h * CH, (h + 1) * CH)
                    k, n, m, j = u % 2, unit(b, h, u), u % KC, 2 * (u // KC)
                    dve.wait_ge(pair_done, n + 1)
                    dve.wait_ge(sum_done, n + 1)
                    nc.vector.scalar_tensor_tensor(t_cos[k][:], pair_ps[k][:, 0, :], bias[:, j, m:m + 1], cos[:, cols],
                                                   ALU.add, ALU.mult).then_inc(cos_done, 1)
                    nc.vector.scalar_tensor_tensor(t_sin[k][:], pair_ps[k][:, 1, :], bias[:, j + 1, m:m + 1], sin[:, cols],
                                                   ALU.add, ALU.mult).then_inc(sin_done, 1)

                def take_rest(b, h, u):
                    k, n = u % 2, unit(b, h, u)
                    dve.wait_ge(part_done[0], n + 1)
                    dve.wait_ge(part_done[2], n + 1)
                    nc.vector.tensor_tensor(rest[k][:], t_sum[k][:], parts[u][:, 0, :], ALU.subtract).then_inc(rest_done, 1)

                def step(this, turned, normed):
                    b, h = this
                    dve.wait_ge(v_done, chunk(b, h) + 1)
                    dve.wait_ge(vout_free[h], 16 * NG * (b + 1))
                    nc.vector.tensor_tensor(vout[h][:, :, :, 0:HD], v_ps[:].rearrange("p t (h c) -> p t h c", c=HD),
                                            vbias[:].rearrange("p (h c) -> p h c", c=HD).unsqueeze(1).broadcast_to([P, CT, H, HD]),
                                            ALU.add).then_inc(v_copied, 1)
                    if normed:
                        moments(*normed)
                    turn_by_angle(b, h, 0)
                    turn_by_angle(b, h, 1)
                    take_rest(b, h, 0)
                    if normed:
                        normalize(*normed)
                    turn_by_angle(b, h, 2)
                    take_rest(b, h, 1)
                    if turned:
                        rest_turned(*turned)
                    turn_by_angle(b, h, 3)
                    take_rest(b, h, 2)
                    take_rest(b, h, 3)

                dve.sem_inc(sin_done, AHEAD)
                dve.sem_inc(rest_done, AHEAD)
                dve.sem_inc(v_copied, 1)
                dve.sem_inc(lo_done, 1)
                dve.wait_ge(p.x_in[0], 16)
                moments(0, 0)
                dve.wait_ge(p.x_in[1], 16)
                moments(0, 1)
                normalize(0, 0)
                normalize(0, 1)
                rest_turned(0, 0)
                for load in range(2, len(p.x_in)):
                    dve.wait_ge(p.x_in[load], 16)
                dve.wait_ge(w_in, 16 * (N_LOADS + len(NAMES)))
                dve.wait_ge(v_ones, 2)
                steps(dve, step)

            @block.tensor
            def _(pe):
                def turn(b, h):
                    n = chunk(b, h)
                    pe.wait_ge(xn_done, CT * (n + 1))
                    pe.wait_ge(lo_done, n + 1)
                    for kc in range(KC):
                        for t in range(CT):
                            last = nc.tensor.transpose(t_ps[:, kc, t * P:(t + 1) * P], xn[h][:, t, kc * P:(kc + 1) * P], p.ident[:])
                    last.then_inc(t_done, 1)

                def step(this, turned, normed):
                    b, h = this
                    n = chunk(b, h)
                    pe.wait_ge(lo_done, n + 2)
                    pe.wait_ge(v_copied, n + 1)
                    for t in range(CT):
                        for kc in range(KC):
                            for i, (wh, xh) in enumerate(HALF_PAIRS):
                                last = nc.tensor.matmul(v_ps[:, t, :], xnT[h][xh][:, kc, t * P:(t + 1) * P], w_half[wh][:, 0, kc, :],
                                                        start=kc == 0 and i == 0, stop=kc == KC - 1 and i == 2)
                    last.then_inc(v_done, 1)
                    for u in range(UC):
                        m = u % KC
                        if u == UC - 1 and turned:
                            turn(*turned)
                        pe.wait_ge(sin_done, unit(b, h, u) + 1)
                        for j in range(2):
                            name = 1 + 2 * (u // KC) + j
                            for kc in range(KC):
                                for i, (wh, xh) in enumerate(HALF_PAIRS):
                                    last = nc.tensor.matmul(pair_ps[u % 2][:, j, :], w_half[wh][:, name, kc, m * P:(m + 1) * P], xnT[h][xh][:, kc, :],
                                                            start=kc == 0 and i == 0, stop=kc == KC - 1 and i == 2)
                        last.then_inc(pair_done, 1)

                pe.sem_inc(t_done, AHEAD)
                turn(0, 0)
                pe.wait_ge(lo_made, len(NAMES))
                steps(pe, step)


def attention(p, layer, causal, behind=None):
    nc = p.nc
    q_scr, k_scr, v_scr, att_scr = p.q_scr[layer], p.k_scr[layer], p.v_scr[layer], p.att_scr[layer]
    with ExitStack() as ctx:
        def sb(name, shape, dt=F32):
            return p.sb(f"a{layer}_" + name, shape, dt, ctx)

        def sem(name):
            return p.sem(f"a{layer}_" + name)

        qa = [sb(f"q{s}", [AROWS, GH, S], BF16) for s in range(SETS)]
        ka = [sb(f"k{s}", [AROWS, GH, S], BF16) for s in range(SETS)]
        va = [sb(f"v{s}", [P, ST, GH, VW]) for s in range(SETS)]
        probs = [sb(f"p{j}", [P, GH, S]) for j in range(2)]
        row_max = [sb(f"rmax{s}", [P, GH, ST]) for s in range(SETS)]
        neg_max = sb("negmax", [GH * ST, 2, P], BF16)
        o_sb = sb("o", [P, S])
        rden = sb("rden", [P, ST * GH])
        o_out = sb("oout", [P, ST * GH, HD])
        ring = [p.ps(f"a{layer}_ring{j}", [P, S], ctx) for j in range(2)]
        s_ps = [p.ps(f"a{layer}_s{j}", [P, CH], ctx) for j in range(2)]
        o_ps = p.ps(f"a{layer}_o_ps", [P, S], ctx)

        loaded, ones_set = [sem(f"loaded{s}") for s in range(SETS)], sem("ones_set")
        ring_full, ring_free = sem("ring_full"), sem("ring_free")
        neg_hi_done, neg_in = sem("neg_hi_done"), sem("neg_in")
        s_full, exp_done, pv_done = sem("s_full"), sem("exp_done"), sem("pv_done")
        o_copied, rden_done, stored = sem("o_copied"), sem("rden_done"), sem("stored")

        LOADS = 2 * len(Q_PARTS) + 1
        STEPS = ST * GH
        TURN = 2 * GH
        SCORES = GH * ST
        LEAD = 12 if causal else 6
        MAX_AT = STEPS - LEAD
        OUT_AT = GH + 2
        RG = SCORES + 2
        assert RG % 2 == 0

        def first_q(kt):
            return kt * P if causal else 0

        def banks_of(kt):
            return [(c, max(first_q(kt), c * CH), (c + 1) * CH) for c in range(HALVES) if first_q(kt) < (c + 1) * CH]

        exp_no, add_no = {}, {}
        for kt in range(ST):
            for c, _, _ in banks_of(kt):
                add_no[kt, c] = len(add_no)
            for h in range(GH):
                for c, _, _ in banks_of(kt):
                    exp_no[kt, h, c] = len(exp_no)
        EXPS, ADDS = len(exp_no), len(add_no)
        EXPS_UNTIL = [1 + max(n for (kt, _, _), n in exp_no.items() if kt <= last) for last in range(ST)]
        assert EXPS % 2 == 0

        EARLY = LEAD + TURN
        START = SCORES + 1 + EARLY
        body_steps = list(range(TURN, STEPS)) + list(range(TURN))

        def units_of(n, inner):
            units = [("score", n + LEAD) if n < MAX_AT and inner else ("next", n - MAX_AT if inner else n + LEAD)]
            if n % 2 and n - 1 == MAX_AT:
                units.append(("max", 0))
            if n % 2 and n - 1 == OUT_AT:
                units.append(("out", 0))
            return units

        in_body = [unit for j, n in enumerate(body_steps) for unit in units_of(n, j < STEPS - TURN)]
        place = {unit: n for n, unit in enumerate(in_body)}
        in_last = [unit for unit in in_body if unit[0] != "next"]
        last_place = {unit: n for n, unit in enumerate(in_last)}
        assert len(in_body) == RG and LEAD % 2 == 0 and TURN % 2 == 0

        END = START + (GROUPS - 2) * RG + len(in_last)

        def slot(number):
            return ring[number % 2]

        with nc.Block() as block:
            @block.sync
            def _(sp):
                def load(g, s):
                    rows = bass.ds(g * GD, GD)
                    for j in range(len(Q_PARTS)):
                        for t, scr, part in ((qa[s], q_scr, Q_PARTS[j]), (ka[s], k_scr, K_PARTS[j])):
                            sp.dma_start(t[j * HD:(j + 1) * HD, :, :],
                                         scr[part, rows, :].rearrange("(h d) t -> d h t", d=HD)).then_inc(loaded[s], 16)
                    sp.dma_start(va[s][:].rearrange("p t h c -> p t (h c)"),
                                 v_scr[bass.ds(g, 1), :, :].rearrange("o (t p) c -> p (o t) c", p=P)).then_inc(loaded[s], 16)

                def place_max(units_before, s):
                    wait_apart(p, sp, ring_free, units_before + 1 + AHEAD)
                    for j in range(2):
                        sp.dma_start(qa[s][SROWS + j:SROWS + j + 1, :, :].rearrange("o h (t q) -> o (h t) q", q=P),
                                     neg_max[:, j, :]).then_inc(neg_in, 16)

                def store(g, units_before):
                    wait_apart(p, sp, ring_free, units_before + 1 + AHEAD)
                    sp.dma_start(att_scr[bass.ds(g, 1), :, :].rearrange("o (t p) c -> p (o t) c", p=P),
                                 o_out[:].rearrange("p (t h) c -> p t (h c)", h=GH)).then_inc(stored, 16)

                def body(g, k, more, where):
                    place_max(START + g * RG + where["max", 0], (k + 1) % SETS)
                    if more:
                        wait_apart(p, sp, pv_done, ADDS * (g + 1))
                        load(g + SETS, k)
                    store(g, START + g * RG + where["out", 0])

                sp.sem_inc(stored, 16)
                sp.sem_inc(neg_in, 32)
                for g in range(SETS):
                    load(g, g)
                place_max(SCORES, 0)
                with sp.Fori(0, (GROUPS - SETS) // SETS) as i:
                    for k in range(SETS):
                        body(i * SETS + k, k, True, place)
                for g in range((GROUPS - SETS) // SETS * SETS, GROUPS - 1):
                    body(g, g % SETS, g + SETS < GROUPS, last_place if g == GROUPS - 2 else place)
                store(GROUPS - 1, END)
                sp.wait_ge(stored, 16 * (GROUPS + 1))

            @block.gpsimd
            def _(pool):
                for s in range(SETS):
                    nc.gpsimd.memset(ka[s][SROWS:AROWS, :, :], 1.0).then_inc(ones_set, 1)
                    pool.wait_ge(ones_set, s + 1)
                if behind:
                    behind.prepare(pool)

            @block.scalar
            def _(act):
                def exps(g, kt, before=None, heads=range(GH)):
                    if heads[0] == 0 and kt >= 2:
                        act.wait_ge(pv_done, ADDS * g + add_no[kt - 2, HALVES - 1] + 1)
                    elif heads[0] == 0 and before is not None:
                        act.wait_ge(pv_done, ADDS * before + add_no[ST - 2 + kt, HALVES - 1] + 1)
                    for h in heads:
                        for c, lo, hi in banks_of(kt):
                            n = exp_no[kt, h, c]
                            act.wait_ge(s_full, EXPS * g + n + 1)
                            nc.scalar.activation(probs[kt % 2][:, h, lo:hi], s_ps[n % 2][:, lo - c * CH:hi - c * CH], ACT.Exp,
                                                 scale=SCALE).then_inc(exp_done, 1)

                def copy_o(g, c):
                    kt = max(kt for kt, bank in add_no if bank == c)
                    act.wait_ge(pv_done, ADDS * g + add_no[kt, c] + 1)
                    nc.scalar.copy(o_sb[:, c * CH:(c + 1) * CH], o_ps[:, c * CH:(c + 1) * CH]).then_inc(o_copied, 1)

                act.sem_inc(exp_done, AHEAD)
                act.sem_inc(o_copied, HALVES)
                exps(0, 0)
                exps(0, 1)
                with act.Fori(0, GROUPS - 1) as g:
                    for kt in range(2, ST):
                        exps(g, kt)
                    exps(g + 1, 0, g)
                    copy_o(g, 0)
                    exps(g + 1, 1, g, range(2))
                    copy_o(g, 1)
                    exps(g + 1, 1, g, range(2, GH))
                for kt in range(2, ST):
                    exps(GROUPS - 1, kt)
                for c in range(HALVES):
                    copy_o(GROUPS - 1, c)

            @block.vector
            def _(dve):
                def maximum(s, u, number, ps):
                    qt, h = divmod(u, GH)
                    dve.wait_ge(ring_full, number + 1)
                    width = (qt + 1) * P if causal else S
                    nc.vector.tensor_reduce(row_max[s][:, h, qt:qt + 1], ps[:, 0:width], AX.X, ALU.max).then_inc(ring_free, 1)

                def negate(g_of, number, ps):
                    dve.wait_ge(ring_full, number + 1)
                    dve.wait_ge(neg_in, 32 * (g_of + 1))
                    nc.vector.tensor_scalar(neg_max[:, 0, :], ps[0:GH * ST, 0:P], -1.0, None, ALU.mult).then_inc(neg_hi_done, 1)
                    dve.wait_ge(neg_hi_done, g_of + 1)
                    nc.vector.scalar_tensor_tensor(neg_max[:, 1, :], ps[0:GH * ST, 0:P], -1.0, neg_max[:, 0, :],
                                                   ALU.mult, ALU.subtract).then_inc(ring_free, 1)

                def divide(g, number, ps):
                    o_t = ps[:].rearrange("p (n c) -> p n c", c=VW)
                    dve.wait_ge(ring_full, number + 1)
                    dve.wait_ge(stored, 16 * (g + 1))
                    nc.vector.reciprocal(rden[:], o_t[:, :, HD]).then_inc(rden_done, 1)
                    dve.wait_ge(rden_done, g + 1)
                    nc.vector.tensor_tensor(o_out[:], o_t[:, :, 0:HD], rden[:].unsqueeze(2).to_broadcast([P, ST * GH, HD]),
                                            ALU.mult).then_inc(ring_free, 1)

                def body(g, k, units):
                    sets = {"score": (k + 1) % SETS, "next": (k + 2) % SETS}
                    for n, (kind, u) in enumerate(units):
                        number, ps = START + g * RG + n, slot(START + n)
                        if kind == "max":
                            negate(g + 1, number, ps)
                        elif kind == "out":
                            divide(g, number, ps)
                        else:
                            maximum(sets[kind], u, number, ps)

                dve.sem_inc(ring_free, AHEAD)
                for u in range(SCORES):
                    maximum(0, u, u, slot(u))
                negate(0, SCORES, slot(SCORES))
                for u in range(EARLY):
                    maximum(1, u, SCORES + 1 + u, slot(SCORES + 1 + u))
                with dve.Fori(0, (GROUPS - SETS) // SETS) as i:
                    for k in range(SETS):
                        body(i * SETS + k, k, in_body)
                for g in range((GROUPS - SETS) // SETS * SETS, GROUPS - 1):
                    body(g, g % SETS, in_last if g == GROUPS - 2 else in_body)
                divide(GROUPS - 1, END, slot(END))

            @block.tensor
            def _(pe):
                def score(s, u, number, ps):
                    qt, h = divmod(u, GH)
                    width = (qt + 1) * P if causal else S
                    pe.wait_ge(ring_free, number + 1)
                    for lo in range(0, width, CH):
                        hi = min(width, lo + CH)
                        diagonal = causal and hi == width
                        last = nc.tensor.matmul(ps[:, lo:hi], qa[s][0:SROWS, h, qt * P:(qt + 1) * P], ka[s][0:SROWS, h, lo:hi],
                                                start=True, stop=not diagonal)
                    if causal:
                        last = nc.tensor.matmul(ps[:, width - P:width], p.ident_bf[:], p.causal[:, 0, :], start=False, stop=True)
                    last.then_inc(ring_full, 1)

                def turn_max(s, number, ps, read):
                    pe.wait_ge(ring_free, read + AHEAD)
                    pe.wait_ge(ring_free, number + 1)
                    nc.tensor.transpose(ps[0:GH * ST, 0:P], row_max[s][:].rearrange("p h t -> p (h t)"), p.ident[:]).then_inc(ring_full, 1)

                def turn_out(g, number, ps):
                    pe.wait_ge(o_copied, HALVES * (g + 2))
                    pe.wait_ge(ring_free, number + 1)
                    for t in range(ST):
                        last = nc.tensor.transpose(ps[:, t * P:(t + 1) * P], o_sb[:, t * P:(t + 1) * P], p.ident[:])
                    last.then_inc(ring_full, 1)

                def weigh(g, s, kt, c):
                    for bank, lo, hi in banks_of(kt):
                        if bank != c:
                            continue
                        pe.wait_ge(exp_done, EXPS * g + EXPS_UNTIL[kt] + AHEAD)
                        if kt == 0:
                            pe.wait_ge(o_copied, HALVES * g + c + 1)
                        for h in range(GH):
                            last = nc.tensor.matmul(o_ps[h * VW:(h + 1) * VW, lo:hi], va[s][:, kt, h, :], probs[kt % 2][:, h, lo:hi],
                                                    start=kt == 0, stop=kt == (hi // P - 1 if causal else ST - 1))
                        last.then_inc(pv_done, 1)

                def keys_by_queries(g, s, n):
                    kt, h = divmod(n, GH)
                    if n == 0:
                        pe.wait_ge(neg_in, 32 * (g + 2))
                    for c, lo, hi in banks_of(kt):
                        m = exp_no[kt, h, c]
                        pe.wait_ge(exp_done, EXPS * g + m + 1)
                        diagonal = causal and lo == kt * P
                        last = nc.tensor.matmul(s_ps[m % 2][:, lo - c * CH:hi - c * CH], ka[s][:, h, kt * P:(kt + 1) * P],
                                                qa[s][:, h, lo:hi], start=True, stop=not diagonal)
                        if diagonal:
                            last = nc.tensor.matmul(s_ps[m % 2][:, lo - c * CH:lo - c * CH + P], p.ident_bf[:], p.causal[:, 1, :],
                                                    start=False, stop=True)
                        last.then_inc(s_full, 1)

                def steps(g, s, n0, n1, before, between):
                    for n in range(n0, n1, 2):
                        kt, h = divmod(n, GH)
                        keys_by_queries(g, s, n)
                        between(n)
                        between(n + 1)
                        keys_by_queries(g, s, n + 1)
                        if kt:
                            weigh(g, s, kt - 1, h // 2)
                        elif before is not None:
                            weigh(*before, ST - 1, h // 2)

                def body(g, k, i, units):
                    where = {unit: n for n, unit in enumerate(units)}
                    sets = {"score": (k + 1) % SETS, "next": (k + 2) % SETS}

                    def between(inner):
                        def make(n):
                            for unit in units_of(n, inner):
                                if unit not in where:
                                    continue
                                kind, u = unit
                                number, ps = START + g * RG + where[unit], slot(START + where[unit])
                                if kind == "max":
                                    turn_max(sets["score"], number, ps, START + g * RG + where["score", SCORES - 1] + 1)
                                elif kind == "out":
                                    turn_out(g, number, ps)
                                else:
                                    if kind == "next" and u == 0:
                                        pe.wait_ge(loaded[sets[kind]], 16 * LOADS * (i + (k + 2) // SETS + 1))
                                    score(sets[kind], u, number, ps)
                        return make

                    steps(g, k, TURN, STEPS, None, between(True))
                    steps(g + 1, (k + 1) % SETS, 0, TURN, (g, k), between(False))

                def first_between(n):
                    u = n + LEAD
                    score(1, u, SCORES + 1 + u, slot(SCORES + 1 + u))

                pe.wait_ge(ones_set, SETS)
                pe.wait_ge(loaded[0], 16 * LOADS)
                for u in range(SCORES):
                    score(0, u, u, slot(u))
                turn_max(0, SCORES, slot(SCORES), SCORES)
                pe.wait_ge(loaded[1], 16 * LOADS)
                for u in range(LEAD):
                    score(1, u, SCORES + 1 + u, slot(SCORES + 1 + u))
                steps(0, 0, 0, TURN, None, first_between)
                with pe.Fori(0, (GROUPS - SETS) // SETS) as i:
                    for k in range(SETS):
                        body(i * SETS + k, k, i, in_body)
                for g in range((GROUPS - SETS) // SETS * SETS, GROUPS - 1):
                    body(g, g % SETS, g // SETS, in_last if g == GROUPS - 2 else in_body)
                g, k = GROUPS - 1, (GROUPS - 1) % SETS
                steps(g, k, TURN, STEPS, None, lambda n: None)
                for c in range(HALVES):
                    weigh(g, k, ST - 1, c)
                turn_out(g, END, slot(END))


def load_attention(sp, scr, b, h, att, loaded):
    for hg in range(NG):
        sp.dma_start(att[:, :, hg * GD:(hg + 1) * GD],
                     scr[bass.ds(b * NG + hg, 1), h * CH:(h + 1) * CH, :].rearrange("o (t p) c -> p (o t) c", p=P)).then_inc(loaded, 16)


def tile_of(x, n):
    return x[:, bass.ds(n, 1), :].rearrange("p o c -> p (o c)")


def project_ffn(p):
    nc, a = p.nc, p.a
    with ExitStack() as ctx:
        def sb(name, shape, dt=F32):
            return p.sb("f_" + name, shape, dt, ctx)

        def sem(name):
            return p.sem("f_" + name)

        w = {n: sb(f"w_{n}", [P, KC, D]) for n in ("out", "q2", "k2", "v2")}
        ln1, obias = sb("ln1", [P, KC]), sb("obias", [P, D])
        att = [sb(f"att{h}", [P, CT, D]) for h in range(2)]
        attT = [sb(f"attT{h}", [P, KC, CH]) for h in range(2)]
        y = [sb(f"y{h}", [P, CT, D]) for h in range(2)]
        yn = [sb(f"yn{h}", [P, CT, D]) for h in range(2)]
        u = [sb(f"u{h}", [P, CT, D]) for h in range(2)]
        z = [sb(f"z{h}", [P, CT, D]) for h in range(2)]
        zT = [sb(f"zT{h}", [P, KC, CH]) for h in range(2)]
        stats = [[sb(f"stats{j}{h}", [P, CT, 6]) for h in range(2)] for j in range(2)]
        mv = [[sb(f"mv{j}{h}", [P, CT, 2]) for h in range(2)] for j in range(2)]
        scaled, square = [sb(f"scaled{h}", [P, CT]) for h in range(2)], [sb(f"square{h}", [P, CT]) for h in range(2)]
        sd = [[sb(f"sd{j}{h}", [P, CT]) for h in range(2)] for j in range(3)]
        rstd = [[sb(f"rstd{j}{h}", [P, CT]) for h in range(2)] for j in range(3)]
        rest = [sb(f"rest{k}", [P, CH]) for k in range(2)]
        parts = [sb(f"parts{k}", [P, PARTS, CH], BF16) for k in range(2 * KC)]
        vout = [sb(f"v{h}", [P, CT, H, VW]) for h in range(2)]
        attT_ps = p.ps("f_attT_ps", [P, KC, CH], ctx)
        zT_ps = p.ps("f_zT_ps", [P, KC, CH], ctx)
        row_ps = p.ps("f_row_ps", [P, CT, D], ctx)
        unit_ps = [p.ps(f"f_unit_ps{k}", [P, CH], ctx) for k in range(2)]

        w_in, w_scaled, v_ones = sem("w_in"), sem("w_scaled"), sem("v_ones")
        att_in = [sem(f"att_in{h}") for h in range(2)]
        att_turned, attT_done, z_turned, zT_done = sem("att_turned"), sem("attT_done"), sem("z_turned"), sem("zT_done")
        yps_done, y_done, yn_done, x1_done = sem("yps_done"), sem("y_done"), sem("yn_done"), sem("x1_done")
        stats_done, mv_done = [sem(f"stats_done{j}") for j in range(2)], [sem(f"mv_done{j}") for j in range(2)]
        sd_done, rstd_done = [sem(f"sd_done{j}") for j in range(3)], [sem(f"rstd_done{j}") for j in range(3)]
        scaled_done, square_done = sem("scaled_done"), sem("square_done")
        u_done, z_done = sem("u_done"), sem("z_done")
        unit_done, rest_done = sem("unit_done"), sem("rest_done")
        part_done = [sem(f"part{n}_done") for n in range(PARTS)]
        v_done, v_copied = sem("v_done"), sem("v_copied")
        parts_free = [sem(f"parts_free{k}") for k in range(2 * KC)]
        vout_free = [sem(f"vout_free{h}") for h in range(2)]
        u_free = [sem(f"u_free{h}") for h in range(2)]
        zT_free = [sem(f"zT_free{h}") for h in range(2)]
        UC = 2 * KC
        UB = UC * HALVES
        N_LOADS = 6

        def chunk(b, h):
            return b * HALVES + h

        def unit(b, h, i):
            return b * UB + (h * UC + i)

        def steps(eng, step):
            with eng.Fori(0, B - 1) as b:
                step(b, 0, (b, 1), (b + 1, 0))
                step(b, 1, (b + 1, 0), (b + 1, 1))
            step(B - 1, 0, (B - 1, 1), None)
            step(B - 1, 1, None, None)

        with nc.Block() as block:
            @block.sync
            def _(sp):
                def load(b, h):
                    wait_apart(p, sp, att_turned, chunk(b, h) + 1)
                    load_attention(sp, p.att_scr[0], b, h, att[h], att_in[h])

                def step(b, h, ahead):
                    n = chunk(b, h)
                    if ahead:
                        load(*ahead)
                    wait_apart(p, sp, u_done, CT * (n + 1))
                    sp.dma_start(p.u_scr[bass.ds(n * CH, CH), :].rearrange("(t p) c -> p t c", p=P), u[h][:]).then_inc(u_free[h], 16)
                    wait_apart(p, sp, zT_done, n + 2)
                    sp.dma_start(p.zT_scr[:, bass.ds(n * CH, CH)].rearrange("(k p) t -> p k t", p=P), zT[h][:]).then_inc(zT_free[h], 16)
                    wait_apart(p, sp, v_copied, n + 2)
                    store_v(sp, p.v_scr[1], b, h, vout[h], vout_free[h])
                    for i in range(UC):
                        m = i % KC
                        scr = (p.q_scr if i < KC else p.k_scr)[1]
                        wait_apart(p, sp, part_done[2], unit(b, h, i) + 1 + AHEAD)
                        sp.dma_start(scr[:, bass.ds(b * D + m * P, P), h * CH:(h + 1) * CH].rearrange("a r t -> r a t"),
                                     parts[i][:]).then_inc(parts_free[i], 16)

                for i in range(UC):
                    sp.sem_inc(parts_free[i], 16)
                for h in range(2):
                    sp.sem_inc(u_free[h], 16)
                    sp.sem_inc(zT_free[h], 16)
                    sp.sem_inc(vout_free[h], 16 * NG)
                for h in range(HALVES):
                    load_attention(sp, p.att_scr[0], 0, h, att[h], att_in[h])
                load(1, 0)
                with sp.Fori(0, B - 2) as b:
                    step(b, 0, (b + 1, 1))
                    step(b, 1, (b + 2, 0))
                step(B - 2, 0, (B - 1, 1))
                step(B - 2, 1, None)
                step(B - 1, 0, None)
                step(B - 1, 1, None)
                for i in range(UC):
                    wait_apart(p, sp, parts_free[i], 16 * (B * HALVES + 1))
                for h in range(2):
                    wait_apart(p, sp, vout_free[h], 16 * NG * (B + 1))
                    wait_apart(p, sp, u_free[h], 16 * (B + 1))
                    wait_apart(p, sp, zT_free[h], 16 * (B + 1))

            @block.gpsimd
            def _(pool):
                def residual(b, h):
                    for t in range(CT):
                        tile = chunk(b, h) * CT + t
                        pool.wait_ge(yn_done, tile + 1 + CT * AHEAD)
                        nc.gpsimd.tensor_tensor(tile_of(p.x_all, tile), tile_of(p.x_all, tile), yn[h][:, t, :], ALU.add).then_inc(x1_done, 1)

                def last_parts(b, h, units):
                    for i in units:
                        pool.wait_ge(part_done[1], unit(b, h, i) + 1)
                        nc.gpsimd.tensor_tensor(parts[i][:, 2, :], rest[i % 2][:], parts[i][:, 1, :], ALU.subtract).then_inc(part_done[2], 1)

                def step(b, h, norms, front):
                    if norms:
                        residual(*norms)
                    last_parts(b, h, range(UC))

                for h in range(2):
                    nc.gpsimd.memset(vout[h][:], 1.0).then_inc(v_ones, 1)
                pool.sem_inc(part_done[2], AHEAD)
                residual(0, 0)
                steps(pool, step)

            @block.scalar
            def _(act):
                for n in ("out", "q2", "k2", "v2"):
                    act.dma_start(w[n][:], rows_in(a["w_" + n])).then_inc(w_in, 16)
                act.dma_start(ln1[:], a["ln1"]).then_inc(w_in, 16)
                act.dma_start(obias[:], a["out_bias"]).then_inc(w_in, 16)

                def root(b, h, j):
                    if j < 2:
                        act.wait_ge(mv_done[j], CT * (chunk(b, h) + 1))
                        nc.scalar.activation(sd[j][h][:], mv[j][h][:, :, 1], ACT.Sqrt, bias=p.eps[:, 0:1]).then_inc(sd_done[j], 1)
                    else:
                        act.wait_ge(square_done, chunk(b, h) + 1)
                        nc.scalar.activation(sd[j][h][:], square[h][:], ACT.Sqrt, bias=p.eps[:, 1:2]).then_inc(sd_done[j], 1)

                def scale_z(b, h):
                    n = chunk(b, h)
                    act.wait_ge(rstd_done[2], n + 1)
                    act.wait_ge(u_done, CT * (n + 1))
                    act.wait_ge(z_turned, n + 1)
                    for t in range(CT):
                        nc.scalar.activation(z[h][:, t, :], u[h][:, t, :], ACT.Copy, scale=rstd[2][h][:, t:t + 1]).then_inc(z_done, 1)

                def front_copy(b, h):
                    act.wait_ge(att_turned, chunk(b, h) + 1 + AHEAD)
                    nc.scalar.copy(attT[h][:], attT_ps[:]).then_inc(attT_done, 1)

                def split(b, h, i):
                    k, n = i % 2, unit(b, h, i)
                    act.wait_ge(parts_free[i], 16 * (chunk(b, h) + 1))
                    act.wait_ge(unit_done, n + 1)
                    nc.scalar.copy(parts[i][:, 0, :], unit_ps[k][:]).then_inc(part_done[0], 1)
                    act.wait_ge(rest_done, n + 1 + AHEAD)
                    nc.scalar.copy(parts[i][:, 1, :], rest[k][:]).then_inc(part_done[1], 1)

                def step(b, h, norms, front):
                    act.wait_ge(zT_free[h], 16 * (b + 1))
                    act.wait_ge(z_turned, chunk(b, h) + 1 + AHEAD)
                    nc.scalar.copy(zT[h][:], zT_ps[:]).then_inc(zT_done, 1)
                    if norms:
                        root(*norms, 0)
                    if front:
                        front_copy(*front)
                    if norms:
                        root(*norms, 1)
                    split(b, h, 0)
                    split(b, h, 1)
                    if norms:
                        root(*norms, 2)
                    split(b, h, 2)
                    if norms:
                        scale_z(*norms)
                    split(b, h, 3)

                act.sem_inc(attT_done, 1)
                act.sem_inc(zT_done, 1)
                for h in range(HALVES):
                    front_copy(0, h)
                for j in range(3):
                    root(0, 0, j)
                scale_z(0, 0)
                steps(act, step)

            @block.vector
            def _(dve):
                def moments(b, h, j, src, ready):
                    n = chunk(b, h)
                    for t in range(CT):
                        if ready is not None:
                            dve.wait_ge(ready, n * CT + t + 1)
                        nc.vector.bn_stats(stats[j][h][:, t, :], src(n * CT + t, t)).then_inc(stats_done[j], 1)
                    wait_apart(p, dve, stats_done[j], CT * (n + 1))
                    for t in range(CT):
                        nc.vector.bn_aggr(mv[j][h][:, t, :], stats[j][h][:, t, :]).then_inc(mv_done[j], 1)

                def invert(b, h, j):
                    n = chunk(b, h)
                    dve.wait_ge(sd_done[j], n + 1)
                    nc.vector.reciprocal(rstd[j][h][:], sd[j][h][:]).then_inc(rstd_done[j], 1)

                def take_y(b, h):
                    n = chunk(b, h)
                    dve.wait_ge(yps_done, n + 1)
                    dve.wait_ge(yn_done, CT * (n + 1))
                    nc.vector.tensor_tensor(y[h][:], row_ps[:], obias[:].unsqueeze(1).broadcast_to([P, CT, D]), ALU.add).then_inc(y_done, 1)
                    dve.wait_ge(y_done, n + 2)
                    moments(b, h, 0, lambda tile, t: y[h][:, t, :], None)

                def norm_y(b, h):
                    n = chunk(b, h)
                    invert(b, h, 0)
                    dve.wait_ge(rstd_done[0], n + 1)
                    for t in range(CT):
                        nc.vector.tensor_scalar(yn[h][:, t, :], y[h][:, t, :], mv[0][h][:, t, 0:1], rstd[0][h][:, t:t + 1],
                                                ALU.subtract, ALU.mult).then_inc(yn_done, 1)

                def norm_x1(b, h):
                    n = chunk(b, h)
                    invert(b, h, 1)
                    dve.wait_ge(rstd_done[1], n + 1)
                    nc.vector.tensor_tensor(scaled[h][:], mv[1][h][:, :, 1], rstd[1][h][:], ALU.mult).then_inc(scaled_done, 1)
                    dve.wait_ge(scaled_done, n + 1)
                    nc.vector.tensor_tensor(square[h][:], scaled[h][:], rstd[1][h][:], ALU.mult).then_inc(square_done, 1)
                    dve.wait_ge(u_free[h], 16 * (b + 1))
                    for t in range(CT):
                        nc.vector.tensor_scalar(u[h][:, t, :], tile_of(p.x_all, n * CT + t), mv[1][h][:, t, 0:1],
                                                rstd[1][h][:, t:t + 1], ALU.subtract, ALU.mult).then_inc(u_done, 1)

                def take_rest(b, h, i):
                    k, n = i % 2, unit(b, h, i)
                    dve.wait_ge(part_done[0], n + 1)
                    dve.wait_ge(part_done[2], n + 1)
                    nc.vector.tensor_tensor(rest[k][:], unit_ps[k][:], parts[i][:, 0, :], ALU.subtract).then_inc(rest_done, 1)

                def step(b, h, norms, front):
                    if norms:
                        norm_y(*norms)
                        moments(*norms, 1, lambda tile, t: tile_of(p.x_all, tile), x1_done)
                    n = chunk(b, h)
                    dve.wait_ge(v_done, n + 1)
                    dve.wait_ge(vout_free[h], 16 * NG * (b + 1))
                    nc.vector.tensor_copy(vout[h][:, :, :, 0:HD], row_ps[:].rearrange("p t (h c) -> p t h c", c=HD)).then_inc(v_copied, 1)
                    take_rest(b, h, 0)
                    if norms:
                        norm_x1(*norms)
                    take_rest(b, h, 1)
                    take_rest(b, h, 2)
                    if norms:
                        invert(*norms, 2)
                    take_rest(b, h, 3)
                    if front:
                        take_y(*front)

                dve.sem_inc(v_copied, 1)
                dve.sem_inc(yn_done, CT * AHEAD)
                dve.sem_inc(y_done, 1)
                dve.sem_inc(rest_done, AHEAD)
                dve.wait_ge(v_ones, 2)
                dve.wait_ge(w_in, 16 * N_LOADS)
                for name in ("q2", "k2", "v2"):
                    for kc in range(KC):
                        nc.vector.tensor_scalar(w[name][:, kc, :], w[name][:, kc, :], ln1[:, kc:kc + 1], None, ALU.mult).then_inc(w_scaled, 1)
                for h in range(HALVES):
                    take_y(0, h)
                norm_y(0, 0)
                moments(0, 0, 1, lambda tile, t: tile_of(p.x_all, tile), x1_done)
                norm_x1(0, 0)
                invert(0, 0, 2)
                steps(dve, step)

            @block.tensor
            def _(pe):
                def turn(ps, src, done):
                    for kc in range(KC):
                        for t in range(CT):
                            last = nc.tensor.transpose(ps[:, kc, t * P:(t + 1) * P], src[:, t, kc * P:(kc + 1) * P], p.ident[:])
                    last.then_inc(done, 1)

                def turn_att(b, h):
                    pe.wait_ge(att_in[h], 16 * NG * (b + 1))
                    pe.wait_ge(attT_done, chunk(b, h) + 1)
                    turn(attT_ps, att[h], att_turned)

                def by_tokens(srcT, weight, done):
                    for t in range(CT):
                        for kc in range(KC):
                            last = nc.tensor.matmul(row_ps[:, t, :], srcT[:, kc, t * P:(t + 1) * P], weight[:, kc, :],
                                                    start=kc == 0, stop=kc == KC - 1)
                    last.then_inc(done, 1)

                def project_out(b, h, v_before):
                    pe.wait_ge(attT_done, chunk(b, h) + 2)
                    pe.wait_ge(y_done, chunk(b, h) + 1)
                    pe.wait_ge(v_copied, v_before)
                    by_tokens(attT[h], w["out"], yps_done)

                def step(b, h, norms, front):
                    n = chunk(b, h)
                    pe.wait_ge(z_done, CT * (n + 1))
                    pe.wait_ge(zT_done, n + 1)
                    turn(zT_ps, z[h], z_turned)
                    if front:
                        turn_att(*front)
                    pe.wait_ge(zT_done, n + 2)
                    pe.wait_ge(y_done, n + 3 if norms else n + 2)
                    pe.wait_ge(v_copied, n + 1)
                    by_tokens(zT[h], w["v2"], v_done)
                    for i in range(UC):
                        m, name = i % KC, ("q2" if i < KC else "k2")
                        pe.wait_ge(rest_done, unit(b, h, i) + 1)
                        for kc in range(KC):
                            last = nc.tensor.matmul(unit_ps[i % 2][:], w[name][:, kc, m * P:(m + 1) * P], zT[h][:, kc, :],
                                                    start=kc == 0, stop=kc == KC - 1)
                        last.then_inc(unit_done, 1)
                    if front:
                        project_out(*front, n + 2)

                pe.sem_inc(att_turned, AHEAD)
                pe.sem_inc(z_turned, AHEAD)
                pe.wait_ge(w_in, 16 * N_LOADS)
                for h in range(HALVES):
                    turn_att(0, h)
                    project_out(0, h, 1)
                pe.wait_ge(w_scaled, 3 * KC)
                steps(pe, step)


class FfnWeights:

    def __init__(self, p, lasting, passing):
        def sb(name, shape, dt=F32, ctx=lasting):
            return p.sb("g_" + name, shape, dt, ctx)

        self.p = p
        shapes = {"gate": [P, KC, F], "up": [P, KC, F], "down": [P, FC, D], "a": [P, KC, P]}
        self.hi = {n: sb(f"hi_{n}", shape, F32R) for n, shape in shapes.items()}
        self.lo = {n: sb(f"lo_{n}", shape, F32R) for n, shape in shapes.items()}
        self.o = sb("w_o", [P, KC, D])
        self.a = sb("a_rep", [P, KC, REPS, R])
        self.b = sb("b_parts", [P, F], BF16)
        self.ln2 = sb("ln2", [P, KC], F32, passing)
        self.a_in = sb("a_in", [P, KC, R], F32, passing)
        self.masks = sb("masks", [P, PARTS], F32, passing)
        self.whole = sb("whole", [P, KC * F], F32, passing)
        self.b_part = [sb(f"b_part{j}", [P, F], BF16, passing) for j in range(PARTS)]
        self.loaded, self.stepped = p.sem("g_w_loaded"), p.sem("g_w_stepped")
        self.steps = 0

    def prepare(self, pool):
        nc, a, whole = self.p.nc, self.p.a, self.whole

        def step(instruction):
            self.steps += 1
            instruction.then_inc(self.stepped, 1)
            pool.wait_ge(self.stepped, self.steps)

        loads = [(self.o[:], rows_in(a["w_o"])), (self.a_in[:], rows_in(a["a"])), (self.ln2[:], a["ln2"]), (self.masks[:], a["b_masks"])]
        for t, src in loads:
            pool.dma_start(t, src).then_inc(self.loaded, 16)
        pool.wait_ge(self.loaded, 16 * len(loads))
        for j, n in enumerate(("gate", "up", "down")):
            src = rows_in(a["w_" + n])
            pool.dma_start(whole[:].rearrange("p (k n) -> p k n", k=src.shape[1]), src).then_inc(self.loaded, 16)
            pool.wait_ge(self.loaded, 16 * (len(loads) + j + 1))
            if n != "down":
                for kc in range(KC):
                    step(nc.gpsimd.tensor_scalar(whole[:, kc * F:(kc + 1) * F], whole[:, kc * F:(kc + 1) * F], self.ln2[:, kc:kc + 1], None, ALU.mult))
            self.split(step, n, whole[:])
        step(nc.gpsimd.tensor_copy(self.a[:], self.a_in[:].unsqueeze(2).broadcast_to([P, KC, REPS, R])))
        for kc in range(KC):
            step(nc.gpsimd.tensor_scalar(whole[:, kc * P:(kc + 1) * P], self.a[:, kc, :, :].rearrange("p r c -> p (r c)"), self.ln2[:, kc:kc + 1], None, ALU.mult))
        self.split(step, "a", whole[:, 0:KC * P])
        rep, rest, part = whole[:, 0:F], whole[:, F:2 * F], self.b_part
        for j in range(REPS):
            pool.dma_start(rep[j * R:(j + 1) * R, :], a["b"]).then_inc(self.loaded, 16)
        pool.wait_ge(self.loaded, 16 * (len(loads) + 3 + REPS))
        step(nc.gpsimd.tensor_copy(part[0][:], rep))
        step(nc.gpsimd.tensor_tensor(rest, rep, part[0][:], ALU.subtract))
        step(nc.gpsimd.tensor_copy(part[1][:], rest))
        step(nc.gpsimd.tensor_tensor(part[2][:], rest, part[1][:], ALU.subtract))
        for j in range(PARTS):
            step(nc.gpsimd.tensor_scalar(part[j][:], part[j][:], self.masks[:, j:j + 1], None, ALU.mult))
        step(nc.gpsimd.tensor_tensor(part[0][:], part[0][:], part[1][:], ALU.add))
        step(nc.gpsimd.tensor_tensor(self.b[:], part[0][:], part[2][:], ALU.add))

    def split(self, step, name, whole):
        hi, lo = (t[name][:].rearrange("p k n -> p (k n)") for t in (self.hi, self.lo))
        step(self.p.nc.gpsimd.tensor_copy(hi, whole))
        step(self.p.nc.gpsimd.tensor_tensor(lo, whole, hi.bitcast(F32), ALU.subtract))

    def products(self, name):
        hi, lo = self.hi[name], self.lo[name]
        return ((hi, 0), (hi, 1), (lo, 0))


def feed_forward(p, w):
    nc = p.nc
    with ExitStack() as ctx:
        def sb(name, shape, dt=F32):
            return p.sb("g_" + name, shape, dt, ctx)

        def sem(name):
            return p.sem("g_" + name)

        woa = sb("woa", [P, KC, P])
        att = [sb(f"att{h}", [P, CT, D]) for h in range(2)]
        attT = sb("attT", [P, KC, CH])
        whole_zT = [sb(f"zT{h}", [P, KC, CH]) for h in range(2)]
        zT = [[sb(f"zT_{n}{h}", [P, KC, CH], F32R) for n in ("hi", "lo")] for h in range(2)]
        u = [sb(f"u{h}", [P, CT, D]) for h in range(2)]
        mod, modh, modh_rest = sb("mod", [P, CH]), sb("modh", [P, CH]), sb("modh_rest", [P, CH])
        modh_parts = [sb(f"modh_parts{h}", [P, CH], BF16) for h in range(2)]
        modh_mid = sb("modh_mid", [P, CH], BF16)
        silu = [sb(f"silu{j}", [P, CH]) for j in range(2)]
        product = [sb(f"product{j}", [P, CH]) for j in range(2)]
        hidden = [sb(f"hidden_{n}", [P, FC, CH], F32R) for n in ("hi", "lo")]
        m = sb("m", [P, CT, D])
        result = [sb(f"result{h}", [P, CT, D]) for h in range(2)]
        stats, mv = sb("stats", [P, CT, 6]), sb("mv", [P, CT, 2])
        sd, rstd = sb("sd", [P, CT]), sb("rstd", [P, CT])
        t_ps = p.ps("g_t_ps", [P, KC, CH], ctx)
        gate_ps = [p.ps(f"g_gate_ps{j}", [P, CH], ctx) for j in range(2)]
        up_ps = [p.ps(f"g_up_ps{j}", [P, CH], ctx) for j in range(2)]
        down_ps = p.ps("g_down_ps", [P, CT, D], ctx)

        woa_made, woa_done = sem("woa_made"), sem("woa_done")
        chunk_in = [sem(f"chunk_in{h}") for h in range(2)]
        t_done, attT_done, low_done, mod_done, modh_done = (sem(n) for n in ("t_done", "attT_done", "low_done", "mod_done", "modh_done"))
        modh_first, modh_second, modh_packed = sem("modh_first"), sem("modh_second"), sem("modh_packed")
        z_hi_done, z_lo_done = sem("z_hi_done"), sem("z_lo_done")
        gate_done, up_done, silu_done, product_done, hi_done, hidden_done = (
            sem(n) for n in ("gate_done", "up_done", "silu_done", "product_done", "hi_done", "hidden_done"))
        down_done, m_done, stats_done, mv_done, sd_done, rstd_done, mn_done, result_done = (
            sem(n) for n in ("down_done", "m_done", "stats_done", "mv_done", "sd_done", "rstd_done", "mn_done", "result_done"))
        result_free = [sem(f"result_free{h}") for h in range(2)]
        C_LOADS = NG + 2
        BANKS, BT = 2, CT // 2
        Z_AT = FC // 2

        def chunk(b, h):
            return b * HALVES + h

        def chunks(eng, step):
            with eng.Fori(0, B - 1) as b:
                step((b, 0), (b, 1))
                step((b, 1), (b + 1, 0))
            step((B - 1, 0), (B - 1, 1))
            step((B - 1, 1), None)

        with nc.Block() as block:
            @block.sync
            def _(sp):
                def load(b, h):
                    n = chunk(b, h)
                    load_attention(sp, p.att_scr[1], b, h, att[h], chunk_in[h])
                    sp.dma_start(whole_zT[h][:], p.zT_scr[:, bass.ds(n * CH, CH)].rearrange("(k p) t -> p k t", p=P)).then_inc(chunk_in[h], 16)
                    sp.dma_start(u[h][:], p.u_scr[bass.ds(n * CH, CH), :].rearrange("(t p) c -> p t c", p=P)).then_inc(chunk_in[h], 16)

                def store(b, h):
                    wait_apart(p, sp, result_done, CT * (chunk(b, h) + 2))
                    sp.dma_start(p.out[bass.ds(chunk(b, h) * CH, CH), :].rearrange("(t p) c -> p t c", p=P), result[h][:]).then_inc(result_free[h], 16)

                for h in range(2):
                    sp.sem_inc(result_free[h], 16)
                load(0, 0)
                load(0, 1)
                with sp.Fori(0, B - 1) as b:
                    for h in range(HALVES):
                        wait_apart(p, sp, m_done, BANKS * (chunk(b, h) + 1))
                        load(b + 1, h)
                        store(b, h)
                store(B - 1, 0)
                store(B - 1, 1)
                for h in range(2):
                    wait_apart(p, sp, result_free[h], 16 * (B + 1))

            @block.gpsimd
            def _(pool):
                def z_lo(b, h):
                    pool.wait_ge(z_hi_done, chunk(b, h) + 1)
                    nc.gpsimd.tensor_tensor(zT[h][1][:], whole_zT[h][:], zT[h][0][:].bitcast(F32), ALU.subtract).then_inc(z_lo_done, 1)

                def step(this, following):
                    b, h = this
                    for f in range(FC):
                        if f == Z_AT and following:
                            z_lo(*following)
                        pool.wait_ge(hi_done, chunk(b, h) * FC + f + 1)
                        nc.gpsimd.tensor_tensor(hidden[1][:, f, :], product[f % 2][:], hidden[0][:, f, :].bitcast(F32), ALU.subtract).then_inc(hidden_done, 1)
                    pool.wait_ge(result_free[h], 16 * (b + 1))
                    for t in range(CT):
                        tile = chunk(b, h) * CT + t
                        pool.wait_ge(mn_done, tile + 1 + CT)
                        nc.gpsimd.tensor_tensor(result[h][:, t, :], tile_of(p.x_all, tile), m[:, t, :], ALU.add).then_inc(result_done, 1)

                pool.sem_inc(result_done, CT)
                pool.sem_inc(hidden_done, AHEAD)
                z_lo(0, 0)
                chunks(pool, step)

            @block.scalar
            def _(act):
                def z_hi(b, h):
                    act.wait_ge(chunk_in[h], 16 * C_LOADS * (b + 1))
                    nc.scalar.copy(zT[h][0][:], whole_zT[h][:]).then_inc(z_hi_done, 1)

                def gate(b, h, f):
                    n = chunk(b, h) * FC + f
                    act.wait_ge(gate_done, n + 1)
                    act.wait_ge(product_done, n + 1)
                    nc.scalar.activation(silu[f % 2][:], gate_ps[f % 2][:], ACT.Silu).then_inc(silu_done, 1)

                def round_hidden(b, h, f):
                    n = chunk(b, h)
                    act.wait_ge(product_done, n * FC + f + 1 + AHEAD)
                    if f == 0:
                        act.wait_ge(down_done, BANKS * (n + 1))
                    nc.scalar.copy(hidden[0][:, f, :], product[f % 2][:]).then_inc(hi_done, 1)

                def turned(b, h):
                    act.wait_ge(t_done, chunk(b, h) + 1)
                    nc.scalar.copy(attT[:], t_ps[:]).then_inc(attT_done, 1)

                def modulate(b, h):
                    act.wait_ge(low_done, chunk(b, h) + 1)
                    act.wait_ge(modh_done, chunk(b, h) + 1)
                    nc.scalar.activation(mod[:], t_ps[:, 0, :], ACT.Tanh).then_inc(mod_done, 1)

                def step(this, following):
                    for f in range(FC):
                        if f == Z_AT and following:
                            z_hi(*following)
                        gate(*this, f)
                        if f:
                            round_hidden(*this, f - 1)
                        if f == FC - 2 and following:
                            turned(*following)
                    round_hidden(*this, FC - 1)
                    if following:
                        modulate(*following)
                    act.wait_ge(mv_done, CT * (chunk(*this) + 1))
                    nc.scalar.activation(sd[:], mv[:, :, 1], ACT.Sqrt, bias=p.eps[:, 0:1]).then_inc(sd_done, 1)

                act.wait_ge(woa_made, 1)
                nc.scalar.copy(woa[:], t_ps[:, :, 0:P]).then_inc(woa_done, 1)
                turned(0, 0)
                z_hi(0, 0)
                modulate(0, 0)
                chunks(act, step)

            @block.vector
            def _(dve):
                def modulate(b, h):
                    n = chunk(b, h)
                    parts = modh_parts[h]
                    dve.wait_ge(mod_done, n + 1)
                    nc.vector.scalar_tensor_tensor(modh[:], mod[:], MOD_SCALE, t_ps[:, 1, :], ALU.mult, ALU.mult).then_inc(modh_done, 1)
                    dve.wait_ge(modh_done, n + 2)
                    nc.vector.tensor_copy(parts[:], modh[:]).then_inc(modh_first, 1)
                    dve.wait_ge(modh_first, n + 1)
                    nc.vector.tensor_tensor(modh_rest[:], modh[:], parts[:], ALU.subtract).then_inc(modh_second, 1)
                    dve.wait_ge(modh_second, 3 * n + 1)
                    nc.vector.tensor_copy(modh_mid[Q3, :], modh_rest[Q3, :]).then_inc(modh_second, 1)
                    nc.vector.tensor_copy(parts[Q1, :], modh_rest[Q1, :]).then_inc(modh_second, 1)
                    dve.wait_ge(modh_second, 3 * n + 3)
                    nc.vector.tensor_tensor(parts[Q3, :], modh_rest[Q3, :], modh_mid[Q3, :], ALU.subtract).then_inc(modh_packed, 1)

                def step(this, following):
                    b, h = this
                    c = chunk(b, h)
                    for f in range(FC):
                        n = c * FC + f
                        dve.wait_ge(up_done, n + 1)
                        dve.wait_ge(silu_done, n + 1)
                        dve.wait_ge(hidden_done, n + 1)
                        nc.vector.tensor_tensor(product[f % 2][:], silu[f % 2][:], up_ps[f % 2][:], ALU.mult).then_inc(product_done, 1)
                    if following:
                        modulate(*following)
                    dve.wait_ge(result_done, CT * (c + 1))
                    for j in range(BANKS):
                        tiles = slice(j * BT, (j + 1) * BT)
                        dve.wait_ge(down_done, BANKS * (c + 1) + j + 1)
                        nc.vector.tensor_tensor(m[:, tiles, :], down_ps[:, tiles, :], u[h][:, tiles, :], ALU.add).then_inc(m_done, 1)
                        dve.wait_ge(m_done, BANKS * c + j + 1)
                        for t in range(j * BT, (j + 1) * BT):
                            nc.vector.bn_stats(stats[:, t, :], m[:, t, :]).then_inc(stats_done, 1)
                        wait_apart(p, dve, stats_done, CT * c + (j + 1) * BT)
                        for t in range(j * BT, (j + 1) * BT):
                            nc.vector.bn_aggr(mv[:, t, :], stats[:, t, :]).then_inc(mv_done, 1)
                    dve.wait_ge(sd_done, c + 1)
                    nc.vector.reciprocal(rstd[:], sd[:]).then_inc(rstd_done, 1)
                    dve.wait_ge(rstd_done, c + 1)
                    for t in range(CT):
                        nc.vector.tensor_scalar(m[:, t, :], m[:, t, :], mv[:, t, 0:1], rstd[:, t:t + 1], ALU.subtract, ALU.mult).then_inc(mn_done, 1)

                dve.sem_inc(modh_done, 1)
                dve.sem_inc(mn_done, CT)
                dve.sem_inc(product_done, AHEAD)
                modulate(0, 0)
                chunks(dve, step)

            @block.tensor
            def _(pe):
                def turn(b, h):
                    pe.wait_ge(chunk_in[h], 16 * C_LOADS * (b + 1))
                    pe.wait_ge(modh_done, chunk(b, h) + 1)
                    for kc in range(KC):
                        for t in range(CT):
                            last = nc.tensor.transpose(t_ps[:, kc, t * P:(t + 1) * P], att[h][:, t, kc * P:(kc + 1) * P], p.ident[:])
                    last.then_inc(t_done, 1)

                def three(ps, name, cols, sources, start, stop, kc):
                    for j, (weight, half) in enumerate(w.products(name)):
                        last = nc.tensor.matmul(ps, weight[:, kc, cols], sources[half][:, kc, :], start=start and j == 0, stop=stop and j == 2)
                    return last

                def low_rank(b, h):
                    n = chunk(b, h)
                    pe.wait_ge(z_lo_done, n + 1)
                    pe.wait_ge(attT_done, n + 1)
                    for kc in range(KC):
                        nc.tensor.matmul(t_ps[:, 0, :], woa[:, kc, :], attT[:, kc, :], start=kc == 0, stop=kc == KC - 1)
                    for kc in range(KC):
                        last = three(t_ps[:, 1, :], "a", slice(0, P), zT[h], kc == 0, kc == KC - 1, kc)
                    last.then_inc(low_done, 1)

                def step(this, following):
                    b, h = this
                    c = chunk(b, h)
                    for f in range(FC):
                        n, cols = c * FC + f, slice(f * P, (f + 1) * P)
                        if f == FC - 1 and following:
                            turn(*following)
                        pe.wait_ge(product_done, n + 1)
                        for kc in range(KC):
                            three(gate_ps[f % 2][:], "gate", cols, zT[h], kc == 0, False, kc)
                        if f == 0:
                            pe.wait_ge(modh_packed, c + 1)
                        nc.tensor.matmul(gate_ps[f % 2][:], w.b[:, cols], modh_parts[h][:], start=False, stop=True).then_inc(gate_done, 1)
                        for kc in range(KC):
                            last = three(up_ps[f % 2][:], "up", cols, zT[h], kc == 0, kc == KC - 1, kc)
                        last.then_inc(up_done, 1)
                    if following:
                        low_rank(*following)
                    pe.wait_ge(mn_done, CT * (c + 1))
                    for j in range(BANKS):
                        for t in range(j * BT, (j + 1) * BT):
                            for f in range(FC):
                                if t == 0:
                                    pe.wait_ge(hidden_done, c * FC + f + 1 + AHEAD)
                                for i, (weight, half) in enumerate(w.products("down")):
                                    last = nc.tensor.matmul(down_ps[:, t, :], hidden[half][:, f, t * P:(t + 1) * P], weight[:, f, :],
                                                            start=f == 0 and i == 0, stop=f == FC - 1 and i == 2)
                        last.then_inc(down_done, 1)

                pe.sem_inc(down_done, BANKS)
                for kc in range(KC):
                    for ko in range(KC):
                        last = nc.tensor.matmul(t_ps[:, kc, 0:P], w.o[:, ko, kc * P:(kc + 1) * P], w.a[:, ko, :, :].rearrange("p r c -> p (r c)"),
                                                start=ko == 0, stop=ko == KC - 1)
                last.then_inc(woa_made, 1)
                pe.wait_ge(woa_done, 1)
                turn(0, 0)
                low_rank(0, 0)
                chunks(pe, step)


def constant_arrays():
    half = HD // 2
    inv_freq = (1.0 / np.float32(10000.0) ** (np.arange(0, HD, 2, dtype=np.float32) / np.float32(HD))).astype(np.float32)
    freqs = np.arange(S, dtype=np.float32)[None, :] * inv_freq[:, None]
    rows = np.arange(P) % half
    sign = np.where(np.arange(P) % HD < half, np.float32(-1), np.float32(1))[:, None]
    cos = np.cos(freqs)[rows].astype(np.float32)
    sin = (np.sin(freqs)[rows] * sign).astype(np.float32)
    turned = np.arange(D) // HD * HD + (np.arange(D) % HD + half) % HD
    return cos, sin, turned


def part_masks():
    masks = np.zeros((P, PARTS), np.float32)
    for rep, part in enumerate(B_PARTS):
        if part is not None:
            masks[rep * R:(rep + 1) * R, part] = 1
    return masks


def kernel(**inputs):
    from concourse import bacc
    from concourse.bass_utils import run_bass_kernel_spmd

    def attn(n):
        return np.asarray(inputs["L0_attn_" + n])

    def ffn(n):
        return np.asarray(inputs["L0_ffn_" + n])

    def by_partition(v):
        return v.reshape(KC, P).T

    cos, sin, turned = constant_arrays()
    data = {
        "x": attn("x").reshape(B * S, D),
        "w_q": attn("q_w").T, "w_qr": attn("q_w")[turned].T,
        "w_k": attn("k_w").T, "w_kr": attn("k_w")[turned].T,
        "w_v": attn("v_w").T, "w_out": attn("out_w").T,
        "qk_bias": np.stack([by_partition(v) for v in (attn("q_b"), attn("q_b")[turned], attn("k_b"), attn("k_b")[turned])], axis=1),
        "v_bias": np.broadcast_to(attn("v_b"), (P, D)), "out_bias": np.broadcast_to(attn("out_b"), (P, D)),
        "cos": cos, "sin": sin,
        "ln1": by_partition(ffn("ln1_w")), "ln2": by_partition(ffn("ln2_w")),
        "w_q2": ffn("Wq").T, "w_k2": ffn("Wk").T, "w_v2": ffn("Wv").T, "w_o": ffn("Wo"),
        "a": ffn("A"), "b": ffn("B"), "b_masks": part_masks(),
        "w_gate": ffn("W_in_base").T, "w_up": ffn("W_up_base").T, "w_down": ffn("W_down").T,
    }
    nc = bacc.Bacc("TRN2", target_bir_lowering=False, num_devices=1)
    arrays, args = {}, {}
    for name, value in data.items():
        value = np.ascontiguousarray(value)
        arrays["in_" + name] = value
        args[name] = nc.dram_tensor("in_" + name, value.shape, mybir.dt.from_np(value.dtype), kind="ExternalInput").ap()
    out = nc.dram_tensor("out_x", (B * S, D), F32, kind="ExternalOutput").ap()
    build(nc, args, out)
    r = run_bass_kernel_spmd(nc, [arrays], core_ids=[0])
    return r.results[0]["out_x"].reshape(B, S, D)
```
